# Optimizing a Trainium2 kernel written in Bass

```python
import numpy as np
import jax
import jax.numpy as jnp

def _softmax(x, axis=-1):
    return jax.nn.softmax(x, axis=axis)

def _gelu(x):
    return jax.nn.gelu(x, approximate=True)

def _silu(x):
    return jax.nn.silu(x)

def _sigmoid(x):
    return jax.nn.sigmoid(x)

def _layernorm(x, axis=-1, eps=1e-05):
    m = jnp.mean(x, axis=axis, keepdims=True)
    v = jnp.var(x, axis=axis, keepdims=True)
    return (x - m) / jnp.sqrt(v + eps)

def _scatter_add(tgt, idx, src, axis=0):
    return tgt.at[idx].add(src)

def _segment_sum(src, seg, n):
    return jax.ops.segment_sum(src, seg, n)
kernel_name = 'mk_xattn_ffn_d2_seqx_r8_a79cae'

def setup_inputs(seed: int=0):
    np.random.seed(seed)
    _w = jnp.asarray

    def _rec_inputs():
        import jax
        import jax.numpy as jnp
        _rk = jax.random.key(seed)
        x = -0.0002928 + 1 * jax.random.normal(jax.random.fold_in(_rk, 1), (32, 128, 128), jnp.float32)
        _lenS = 128 - jax.random.randint(jax.random.fold_in(_rk, 7), (32,), 0, max(1, 128 // 4) + 1, jnp.int32)
        _lenS2 = 128 - jax.random.randint(jax.random.fold_in(_rk, 8), (32,), 0, max(1, 128 // 4) + 1, jnp.int32)
        _ctx_1024P = jax.random.normal(jax.random.fold_in(_rk, 11), (32, 16, 128), jnp.float32)
        _ctx_1024c = jax.random.dirichlet(jax.random.fold_in(_rk, 511), 0.3 * jnp.ones((16,), jnp.float32), (32, 128))
        _ctx_1024t = jnp.einsum('bsk,bkd->bsd', _ctx_1024c, _ctx_1024P)
        _ctx_1024t = _ctx_1024t * jax.lax.rsqrt(jnp.mean(jnp.square(_ctx_1024t)) + 1e-12) * 0.953939
        ctx_1024 = -1.39393e-06 + 0.999914 * (_ctx_1024t + 0.3 * jax.random.normal(jax.random.fold_in(_rk, 611), (32, 128, 128), jnp.float32))
        _validS = jnp.arange(128)[None, :] < _lenS[:, None]
        _validS2 = jnp.arange(128)[None, :] < _lenS2[:, None]
        _causal = jnp.tril(jnp.ones((128, 128), dtype=bool))
        mask_BxS2_bf1 = jnp.ones((32, 128), dtype=bool)
        mask_BxS_ik0 = jnp.where(jnp.broadcast_to(_validS[:, :], (32, 128)), 0, 1).astype(jnp.int32)
        return (x, ctx_1024, mask_BxS2_bf1, mask_BxS_ik0)
    x, ctx_1024, mask_BxS2_bf1, mask_BxS_ik0 = _rec_inputs()

    def _L0_xattn_setup():
        import jax, jax.numpy as jnp
        import numpy as np
        N_HEADS = 16
        D_MODEL = 128
        HEAD_DIM = D_MODEL // N_HEADS
        MASK_FILL = -100000000.0

        def _split_heads(x):
            B, S, _ = x.shape
            return x.reshape(B, S, N_HEADS, HEAD_DIM).transpose(0, 2, 1, 3)
        key = jax.random.key(seed)
        ks = jax.random.split(key, 12)
        B, L, P = (2, 256, 256)
        s = 1.0 / np.sqrt(D_MODEL).astype(np.float32)
        inp = {'q': jax.random.normal(ks[0], (B, L, D_MODEL), dtype=jnp.float32), 'k': jax.random.normal(ks[1], (B, P, D_MODEL), dtype=jnp.float32), 'v': jax.random.normal(ks[2], (B, P, D_MODEL), dtype=jnp.float32), 'attention_mask': jnp.ones((B, P), dtype=bool), 'Wq': jax.random.normal(ks[3], (D_MODEL, D_MODEL), dtype=jnp.float32) * s, 'bq': jnp.zeros((D_MODEL,), dtype=jnp.float32), 'Wk': jax.random.normal(ks[4], (D_MODEL, D_MODEL), dtype=jnp.float32) * s, 'bk': jnp.zeros((D_MODEL,), dtype=jnp.float32), 'Wv': jax.random.normal(ks[5], (D_MODEL, D_MODEL), dtype=jnp.float32) * s, 'bv': jnp.zeros((D_MODEL,), dtype=jnp.float32), 'Wo': jax.random.normal(ks[6], (D_MODEL, D_MODEL), dtype=jnp.float32) * s, 'bo': jnp.zeros((D_MODEL,), dtype=jnp.float32)}
        return inp
    _L0_xattn_all = _L0_xattn_setup()
    _L0_xattn_in = {k: v for k, v in _L0_xattn_all.items() if k in ('Wq', 'bq', 'Wk', 'bk', 'Wv', 'bv', 'Wo', 'bo')}
    del _L0_xattn_all

    def _L0_ffn_setup():
        import jax, jax.numpy as jnp
        import numpy as np
        TOP_K = 2
        key = jax.random.key(seed)
        k1, k2, k3, k4 = jax.random.split(key, 4)
        B, S, D, E = (4, 256, 128, 8)
        x = jax.random.normal(k1, (B, S, D), dtype=jnp.float32)
        w_gate = jax.random.normal(k2, (D, E), dtype=jnp.float32) * 0.02
        w1 = jax.random.normal(k3, (E, D, 4 * D), dtype=jnp.float32) * 0.02
        w2 = jax.random.normal(k4, (E, 4 * D, D), dtype=jnp.float32) * 0.02
        return {'x': x, 'w_gate': w_gate, 'w1': w1, 'w2': w2}
    _L0_ffn_all = _L0_ffn_setup()
    _L0_ffn_in = {k: v for k, v in _L0_ffn_all.items() if k in ('w_gate', 'w1', 'w2')}
    del _L0_ffn_all

    def _L1_xattn_setup():
        import jax, jax.numpy as jnp
        import numpy as np
        HEADS = 16
        DIM_HEAD = 64
        SCALE = DIM_HEAD ** (-0.5)
        MASK_NEG = 1000000.0

        def _split_heads(t):
            b, n, _ = t.shape
            return t.reshape(b, n, HEADS, DIM_HEAD).transpose(0, 2, 1, 3)
        key = jax.random.key(seed)
        ks = jax.random.split(key, 6)
        B, N, M, D = (2, 256, 256, 128)
        inner = HEADS * DIM_HEAD
        x = jax.random.normal(ks[0], (B, N, D), dtype=jnp.float32)
        context = jax.random.normal(ks[1], (B, M, D), dtype=jnp.float32)
        mask = jax.random.randint(ks[2], (B, N), 0, 2, dtype=jnp.int32)
        Wq = jax.random.normal(ks[3], (D, inner), dtype=jnp.float32) * D ** (-0.5)
        Wkv = jax.random.normal(ks[4], (D, 2 * inner), dtype=jnp.float32) * D ** (-0.5)
        Wout = jax.random.normal(ks[5], (inner, D), dtype=jnp.float32) * inner ** (-0.5)
        bout = jnp.zeros((D,), dtype=jnp.float32)
        return {'x': x, 'context': context, 'mask': mask, 'Wq': Wq, 'Wkv': Wkv, 'Wout': Wout, 'bout': bout}
    _L1_xattn_all = _L1_xattn_setup()
    _L1_xattn_in = {k: v for k, v in _L1_xattn_all.items() if k in ('Wq', 'Wkv', 'Wout', 'bout')}
    del _L1_xattn_all

    def _L1_ffn_setup():
        import jax, jax.numpy as jnp
        import numpy as np
        B, S, D = (4, 256, 128)
        N_EXPERTS, EXPERT_SIZE = (16, 32)
        WIDTH = N_EXPERTS * EXPERT_SIZE
        key = jax.random.key(seed)
        k_x, k_w1, k_w2, k_g = jax.random.split(key, 4)
        x = jax.random.normal(k_x, (B, S, D), dtype=jnp.float32)
        w1 = jax.random.normal(k_w1, (D, WIDTH), dtype=jnp.float32) / np.sqrt(D).astype(np.float32)
        b1 = jnp.zeros((WIDTH,), dtype=jnp.float32)
        w2 = jax.random.normal(k_w2, (WIDTH, D), dtype=jnp.float32) / np.sqrt(WIDTH).astype(np.float32)
        b2 = jnp.zeros((D,), dtype=jnp.float32)
        return {'x': x, 'w1': w1, 'b1': b1, 'w2': w2, 'b2': b2}
    _L1_ffn_all = _L1_ffn_setup()
    _L1_ffn_in = {k: v for k, v in _L1_ffn_all.items() if k in ('w1', 'b1', 'w2', 'b2')}
    del _L1_ffn_all
    return {'x': x, 'ctx_1024': ctx_1024, 'mask_BxS2_bf1': mask_BxS2_bf1, 'mask_BxS_ik0': mask_BxS_ik0, 'L0_xattn_Wq': _L0_xattn_in['Wq'], 'L0_xattn_bq': _L0_xattn_in['bq'], 'L0_xattn_Wk': _L0_xattn_in['Wk'], 'L0_xattn_bk': _L0_xattn_in['bk'], 'L0_xattn_Wv': _L0_xattn_in['Wv'], 'L0_xattn_bv': _L0_xattn_in['bv'], 'L0_xattn_Wo': _L0_xattn_in['Wo'], 'L0_xattn_bo': _L0_xattn_in['bo'], 'L0_ffn_w_gate': _L0_ffn_in['w_gate'], 'L0_ffn_w1': _L0_ffn_in['w1'], 'L0_ffn_w2': _L0_ffn_in['w2'], 'L1_xattn_Wq': _L1_xattn_in['Wq'], 'L1_xattn_Wkv': _L1_xattn_in['Wkv'], 'L1_xattn_Wout': _L1_xattn_in['Wout'], 'L1_xattn_bout': _L1_xattn_in['bout'], 'L1_ffn_w1': _L1_ffn_in['w1'], 'L1_ffn_b1': _L1_ffn_in['b1'], 'L1_ffn_w2': _L1_ffn_in['w2'], 'L1_ffn_b2': _L1_ffn_in['b2']}

def reference(x, ctx_1024, mask_BxS2_bf1, mask_BxS_ik0, L0_xattn_Wq, L0_xattn_bq, L0_xattn_Wk, L0_xattn_bk, L0_xattn_Wv, L0_xattn_bv, L0_xattn_Wo, L0_xattn_bo, L0_ffn_w_gate, L0_ffn_w1, L0_ffn_w2, L1_xattn_Wq, L1_xattn_Wkv, L1_xattn_Wout, L1_xattn_bout, L1_ffn_w1, L1_ffn_b1, L1_ffn_w2, L1_ffn_b2):
    import jax
    import jax.numpy as jnp

    def _L0_xattn_ref(q, k, v, attention_mask, Wq, bq, Wk, bk, Wv, bv, Wo, bo):
        import jax, jax.numpy as jnp
        import numpy as np
        N_HEADS = 16
        D_MODEL = 128
        HEAD_DIM = D_MODEL // N_HEADS
        MASK_FILL = -100000000.0

        def _split_heads(x):
            B, S, _ = x.shape
            return x.reshape(B, S, N_HEADS, HEAD_DIM).transpose(0, 2, 1, 3)
        qm = _split_heads(q @ Wq.T + bq)
        km = _split_heads(k @ Wk.T + bk)
        vm = _split_heads(v @ Wv.T + bv)
        scores = jnp.einsum('bnlh,bnph->bnlp', qm, km) / np.sqrt(HEAD_DIM).astype(np.float32)
        mask = attention_mask[:, None, None, :]
        scores = jnp.where(mask, scores, MASK_FILL)
        attn = jax.nn.softmax(scores, axis=-1)
        out = jnp.einsum('bnlp,bnph->bnlh', attn, vm)
        B, _, L, _ = out.shape
        out = out.transpose(0, 2, 1, 3).reshape(B, L, D_MODEL)
        return out @ Wo.T + bo

    def _L0_ffn_ref(x, w_gate, w1, w2):
        import jax, jax.numpy as jnp
        import numpy as np
        TOP_K = 2
        B, S, D = x.shape
        E = w1.shape[0]
        xt = x.reshape(-1, D)
        T = xt.shape[0]
        logits = xt @ w_gate
        topk_vals, topk_idx = jax.lax.top_k(logits, TOP_K)
        gates = jax.nn.softmax(topk_vals, axis=-1)
        comb = jnp.zeros((T, E), dtype=x.dtype)
        comb = comb.at[jnp.arange(T)[:, None], topk_idx].add(gates)
        out = jnp.zeros_like(xt)
        for e in range(E):
            h = jax.nn.relu(xt @ w1[e])
            y = h @ w2[e]
            out = out + comb[:, e:e + 1] * y
        return out.reshape(B, S, D)

    def _L1_xattn_ref(x, context, mask, Wq, Wkv, Wout, bout):
        import jax, jax.numpy as jnp
        import numpy as np
        HEADS = 16
        DIM_HEAD = 64
        SCALE = DIM_HEAD ** (-0.5)
        MASK_NEG = 1000000.0

        def _split_heads(t):
            b, n, _ = t.shape
            return t.reshape(b, n, HEADS, DIM_HEAD).transpose(0, 2, 1, 3)
        kv = context @ Wkv
        k, v = jnp.split(kv, 2, axis=-1)
        q = x @ Wq
        q, k, v = (_split_heads(q), _split_heads(k), _split_heads(v))
        dots = jnp.einsum('bhnd,bhmd->bhnm', q, k) * SCALE
        dots = dots - (1.0 - mask.astype(jnp.float32))[:, None, :, None] * MASK_NEG
        attn = jax.nn.softmax(dots, axis=-1)
        out = jnp.einsum('bhnm,bhmd->bhnd', attn, v)
        b, h, n, d = out.shape
        out = out.transpose(0, 2, 1, 3).reshape(b, n, h * d)
        return out @ Wout + bout

    def _L1_ffn_ref(x, w1, b1, w2, b2):
        import jax, jax.numpy as jnp
        import numpy as np
        B, S, D = (4, 256, 128)
        N_EXPERTS, EXPERT_SIZE = (16, 32)
        WIDTH = N_EXPERTS * EXPERT_SIZE
        h = jax.nn.relu(jnp.einsum('bsd,dw->bsw', x, w1) + b1)
        return jnp.einsum('bsw,wd->bsd', h, w2) + b2
    x = x + _L0_xattn_ref(_layernorm(x, axis=-1), ctx_1024, ctx_1024, mask_BxS2_bf1, L0_xattn_Wq, L0_xattn_bq, L0_xattn_Wk, L0_xattn_bk, L0_xattn_Wv, L0_xattn_bv, L0_xattn_Wo, L0_xattn_bo)
    x = x + _L0_ffn_ref(_layernorm(x, axis=-1), L0_ffn_w_gate, L0_ffn_w1, L0_ffn_w2)
    x = x + _L1_xattn_ref(_layernorm(x, axis=-1), ctx_1024, mask_BxS_ik0, L1_xattn_Wq, L1_xattn_Wkv, L1_xattn_Wout, L1_xattn_bout)
    x = x + _L1_ffn_ref(_layernorm(x, axis=-1), L1_ffn_w1, L1_ffn_b1, L1_ffn_w2, L1_ffn_b2)
    return x

_drawn_inputs = setup_inputs


def setup_inputs(seed=0):
    import zlib

    import numpy as np

    out = dict(_drawn_inputs(seed))
    spreads = {'L0_xattn_bq': (0.0, 0.391),
     'L0_xattn_bk': (0.0, 0.8),
     'L0_xattn_bv': (0.0, 0.1),
     'L0_xattn_bo': (0.0, 0.1),
     'L1_xattn_bout': (0.0, 0.1),
     'L1_ffn_b1': (0.0, 0.1),
     'L1_ffn_b2': (0.0, 0.1)}
    factors = {}
    for name, (base, spread) in spreads.items():
        noise = np.random.default_rng([zlib.crc32(name.encode()), seed]).standard_normal(out[name].shape)
        drawn = base * np.exp(spread * noise) if base else spread * noise
        out[name] = jnp.asarray(drawn.astype(out[name].dtype))
    for name, factor in factors.items():
        out[name] = (out[name] * factor).astype(out[name].dtype)
    return out
```

```python
import concourse.bass as bass
from concourse import mybir
from contextlib import ExitStack

FP32 = mybir.dt.float32
FP32R = mybir.dt.float32r
BF16 = mybir.dt.bfloat16
U8 = mybir.dt.uint8
U32 = mybir.dt.uint32
I32 = mybir.dt.int32
ALU = mybir.AluOpType
ACT = mybir.ActivationFunctionType
AXX = mybir.AxisListType.X

NB = 32
P = 128
NH = 16
G = 4
NU = NH // G
DH0 = P // NH
DH1 = 64
INNER = NH * DH1
PAIRS = INNER // P
NE = 8
HC = 4
REPS = 4
EPS = 1e-5
FILL0 = 1e8
FILL1 = 1e6
MROWS = 64


def bf16_parts(value):
    import numpy as np
    parts, rest = [], np.float32(value)
    for _ in range(3):
        bits = np.array([rest], np.float32).view(np.uint32)
        part = ((bits + 0x7FFF + ((bits >> 16) & 1)) & 0xFFFF0000).astype(np.uint32).view(np.float32)[0]
        parts.append(float(part))
        rest = np.float32(rest - part)
    return parts


def over_items(engine, step):
    for n in (-1, 0, 1):
        step(n, n % 2)
    with engine.Fori(1, NB // 2 - 1) as i:
        step(i * 2, 0)
        step(i * 2 + 1, 1)
    for n in (NB - 2, NB - 1):
        step(n, n % 2)


def loads(m, p):
    return 8 * (m - p) + 16


def has_front(n):
    return not (isinstance(n, int) and n + 1 >= NB)


def has_back(n):
    return not (isinstance(n, int) and n < 0)


def is_start(n):
    return isinstance(n, int) and n == -1


def has_norm(n):
    return not (isinstance(n, int) and n + 2 >= NB)


def wait(engine, semaphore, value):
    if isinstance(value, int) and value <= 0:
        return
    engine.wait_ge(semaphore, value)


def build(nc, x, ctx_in, mask_keys, mask_queries, wq0, bq0, wk0, bk0, wv0, bv0, wo0, bo0,
          gate_w, moe_w1, moe_w2, wq1, wkv1, wout1, bout1, ffn_w1, ffn_b1, ffn_w2, ffn_b2, out):
    ctx = ExitStack()
    with ctx:
        def sb(name, shape, dt=FP32):
            return ctx.enter_context(nc.sbuf_tensor(name, shape, dt))

        def sem(name):
            return ctx.enter_context(nc.semaphore(name))

        ctx.enter_context(nc.allow_non_contiguous_dma(reason="small bias and weight layouts"))
        bank = [ctx.enter_context(nc.psum_tensor(f"bank{i}", [P, 512], FP32)) for i in range(8)]
        S_BANK, T_BANK = bank[0:2], bank[2:4]
        M_BANK = bank[7]

        ident = sb("ident", [P, P])
        identb = sb("identb", [P, P], BF16)
        ones3 = sb("ones3", [3, P], BF16)
        one1 = sb("one1", [1, 1])
        sel = sb("sel", [MROWS, NH + 1, P], BF16)
        expo = sb("expo", [P, 1])
        iota8 = sb("iota8", [P, NE])
        X = sb("X", [P, NB, P])
        nat0 = sb("nat0", [P, 4, P])
        wqk_rep = sb("wqk_rep", [P, 2, NU, P])
        wv0T = sb("wv0T", [P, P])
        wo0T = sb("wo0T", [P, P])
        bqk = sb("bqk", [P, 2, NU])
        patt = sb("patt", [1, 5, P])
        pcol = sb("pcol", [P, 5])
        brow_f = sb("brow_f", [1, 5, 3, P])
        brow_b = sb("brow_b", [1, 4, 3, P], BF16)
        brow = sb("brow", [3, 4, P], BF16)
        mk_u8 = sb("mk_u8", [NB, P], U8)
        mk_bc = sb("mk_bc", [P, NB * P], U8)
        mk_f = sb("mk_f", [NB, 3, P])
        mk3 = sb("mk3", [3, NB * P], U8)
        mk_rows = sb("mk_rows", [3, NB * P], BF16)
        mk_col = sb("mk_col", [P, NB])
        mq_i = sb("mq_i", [NB, P], I32)
        mq_f = sb("mq_f", [NB, 3, P])
        c_col = sb("c_col", [P, NB])
        c_tmp = sb("c_tmp", [P, 3, NB])
        c_parts = sb("c_parts", [P, NB, 3], BF16)
        YT = sb("YT", [P, 2, NH, P])
        nat1 = YT[:, 0, :, :].rearrange("p (i k) s -> p i (k s)", i=2)
        qkT = YT[:, 1, :, :].rearrange("p (i k) s -> p i k s", i=2)
        A = sb("A", [P, NH, P])
        wv1 = sb("wv1", [P, INNER])
        wout = sb("wout", [P, PAIRS, P])
        gw = sb("gw", [P, NE])
        w1 = sb("w1", [P, NE, HC * P])
        w2 = sb("w2", [P, NE, HC, P])
        f1 = sb("f1", [P, HC * P])
        f2 = sb("f2", [P, HC, P])
        fb1 = sb("fb1", [P, HC])
        stats = sb("stats", [P, 2, 6])
        mv = sb("mv", [P, 2, 2])
        veps = sb("veps", [P, 2, 1])
        rstd = sb("rstd", [P, 2, 1])
        XN = sb("XN", [P, 2, P])
        CX = sb("CX", [P, 2, P])
        XCT = sb("XCT", [P, 2, 2, P])
        QF = sb("QF", [P, 2, NU, P])
        HF = sb("HF", [P, 2, NU, P])
        QS = sb("QS", [P, NU, P], FP32R)
        KS = sb("KS", [P, 2, NU, P], FP32R)
        QBD = sb("QBD", [P, 2, NU, G, P], FP32R)
        V0 = sb("V0", [P, 2, NH, DH0 + 1])
        mx = sb("mx", [P, 2, NH])
        mpf = sb("mpf", [P, 3, NH])
        mp = sb("mp", [P, 2, MROWS], BF16)
        MT = sb("MT", [MROWS, 2, P], BF16)
        V1 = sb("V1", [P, 2, NH, DH1 + 1])
        PR = sb("PR", [P, 2, G * P])
        rden = sb("rden", [P, 2, NH])
        ON = sb("ON", [P, 2, G * DH1])
        OT = sb("OT", [P, 2, PAIRS, P])
        H = sb("H", [P, 3, HC, P])
        lg = sb("lg", [P, 2, NE])
        top = sb("top", [P, 2, 8])
        topi = sb("topi", [P, 2, 8], U32)
        topf = sb("topf", [P, 2, 2])
        gcol = sb("gcol", [P, 2, 5])
        comb = sb("comb", [P, 2, 2, NE])
        acc = sb("acc", [P, 2, P])

        ld_setup, ld_w0, ld_w1, ld_ffn, ld_x = (sem(s) for s in ("ld_setup", "ld_w0", "ld_w1", "ld_ffn", "ld_x"))
        const_ready, pool_self, dve_self, act_self = (sem(s) for s in ("const_ready", "pool_self", "dve_self", "act_self"))
        set_pe, set_copy, rows_moved, bd_zeroed = (sem(s) for s in ("set_pe", "set_copy", "rows_moved", "bd_zeroed"))
        parts_ready, out_stored = sem("parts_ready"), [sem("out_stored0"), sem("out_stored1")]

        def wait_apart(engine, *counts):
            counts = [(s, v if isinstance(v, int) else engine.to_reg(v)) for s, v in counts]
            engine.wait_ge(const_ready, 1)
            for s, v in counts:
                wait(engine, s, v)

        def names(prefix, words):
            return {w: sem(f"{prefix}_{w}") for w in words.split()}

        common = "stat var veps rstd xn ctx0 ctx1 tr xct "
        a = names("a", common + "q k v0 qf kf vc hf qs bd ks s mx mp mt mT t e pv on rd ot oT o x mstep")
        c = names("c", common + "v vc y yc s mx mp mt mT t e pv on rd ot oT o x mstep")
        b = names("b", common + "lg lgc top topi topf d e g comb h hr y yacc x step")
        d = names("d", common + "h hr y x")

        block = ctx.enter_context(nc.Block())
        x_v = x.rearrange("b s d -> s b d")
        flat_mask = mask_keys.rearrange("b s -> (b s)")

        def norm_dve_stats(dve, s, prev_x, m, p):
            if prev_x is not None:
                wait(dve, prev_x, m + 1)
            nc.vector.bn_stats(stats[:, p, :], X[:, m, :]).then_inc(s["stat"], 1)
            wait_apart(dve, (s["stat"], m + 1), (s["rstd"], m - 1))
            nc.vector.bn_aggr(mv[:, p, :], stats[:, p, :]).then_inc(s["var"], 1)

        def norm_pool(pool, s, m, p):
            wait_apart(pool, (s["var"], m + 1))
            nc.gpsimd.tensor_scalar(veps[:, p, :], mv[:, p, 1:2], EPS, None, ALU.add).then_inc(s["veps"], 1)
            wait(pool, s["veps"], m + 1)
            wait(pool, s["xn"], m - 1)
            nc.gpsimd.tensor_tensor(rstd[:, p, :], veps[:, p, :], expo[:], ALU.pow).then_inc(s["rstd"], 1)

        def norm_dve_apply(dve, s, m, p):
            wait(dve, s["rstd"], m + 1)
            wait(dve, s["tr"], m - 1)
            nc.vector.tensor_scalar(XN[:, p, :], X[:, m, :], mv[:, p, 0:1], rstd[:, p, :],
                                    ALU.subtract, ALU.mult).then_inc(s["xn"], 1)

        def load_ctx(sp, s, m, p):
            wait(sp, s["tr"], m - 1)
            sp.dma_start(CX[:, p, :], ctx_in[m]).then_inc(s[f"ctx{p}"], 16)

        def max_parts_pool(pool, s, m, p, masked):
            wait_apart(pool, (s["mx"], NU * (m + 1)))
            if masked:
                nc.gpsimd.tensor_tensor(mpf[:, 0, :], c_col[:, bass.ds(m, 1)].broadcast_to([P, NH]), mx[:, p, :],
                                        ALU.subtract).then_inc(s["mstep"], 1)
            else:
                nc.gpsimd.tensor_scalar(mpf[:, 0, :], mx[:, p, :], -1.0, None, ALU.mult).then_inc(s["mstep"], 1)
            wait_apart(pool, (s["mt"], m - 1), (s["mstep"], 4 * m + 1))
            nc.gpsimd.tensor_copy(mp[:, p, 0:NH], mpf[:, 0, :]).then_inc(s["mstep"], 1)
            wait(pool, s["mstep"], 4 * m + 2)
            nc.gpsimd.tensor_tensor(mpf[:, 1, :], mpf[:, 0, :], mp[:, p, 0:NH], ALU.subtract).then_inc(s["mstep"], 1)
            wait_apart(pool, (s["mstep"], 4 * m + 3))
            nc.gpsimd.tensor_copy(mp[:, p, NH:2 * NH], mpf[:, 1, :]).then_inc(s["mstep"], 1)
            wait_apart(pool, (s["mstep"], 4 * m + 4))
            if masked:
                nc.gpsimd.tensor_copy(mp[:, p, 3 * NH:3 * NH + 3], c_parts[:, m, :])
            nc.gpsimd.tensor_tensor(mp[:, p, 2 * NH:3 * NH], mpf[:, 1, :], mp[:, p, NH:2 * NH],
                                    ALU.subtract).then_inc(s["mp"], 1)

        def add_minus_max(s, m, p, g, last_sem, bank_t):
            for j in range(G):
                last = nc.tensor.matmul(bank_t[:, j * P:(j + 1) * P], sel[:, g * G + j, :], MT[:, p, :],
                                        start=False, stop=(j == G - 1), skip_group_check=True)
            last.then_inc(last_sem, 1)

        @block.sync
        def _(sp):
            for src, i in ((wq0, 0), (wk0, 1), (wv0, 2), (wo0, 3)):
                sp.dma_start(nat0[:, i, :], src).then_inc(ld_w0, 16)
            sp.dma_start(mk_u8[:], mask_keys).then_inc(ld_setup, 16)
            sp.dma_start(mq_i[:], mask_queries).then_inc(ld_setup, 16)
            for i, src in enumerate((bv0, bo0, bout1, ffn_b2)):
                sp.dma_start(brow_f[0:1, i, 0, :], src.unsqueeze(0)).then_inc(ld_setup, 16)
            for j in range(G):
                for r in range(REPS):
                    rows = slice((j * REPS + r) * DH0, (j * REPS + r + 1) * DH0)
                    for i, src in enumerate((bq0, bk0)):
                        sp.dma_start(bqk[rows, i, :], src.rearrange("(g j d) -> j d g", g=NU, j=G)[j]).then_inc(ld_setup, 16)
            for k in range(4):
                sp.dma_start(X[:, 8 * k:8 * k + 8, :], x_v[:, 8 * k:8 * k + 8, :]).then_inc(ld_x, 16)
            sp.dma_start(mk_bc[:], flat_mask.partition_broadcast(P)).then_inc(ld_setup, 16)
            sp.dma_start(mk3[:], flat_mask.partition_broadcast(3)).then_inc(ld_setup, 16)
            sp.wait_ge(parts_ready, 2)
            for r in range(3):
                sp.dma_start(brow[r:r + 1, :, :], brow_b[0:1, :, r, :]).then_inc(rows_moved, 16)

            def step0(n, p):
                if has_norm(n):
                    load_ctx(sp, a, n + 2, p)
                if has_front(n):
                    wait_apart(sp, (a["qs"], n + 2), (a["t"], NU * n))
                    for j in range(G):
                        rows = slice(j * REPS * DH0, (j + 1) * REPS * DH0)
                        sp.dma_start(QBD[rows, 1 - p, :, j, :].bitcast(FP32), QS[rows, :, :].bitcast(FP32)).then_inc(a["bd"], 16)

            sp.wait_ge(bd_zeroed, 1)
            load_ctx(sp, a, 0, 0)
            over_items(sp, step0)

            load_ctx(sp, c, 0, 0)

            def step1(n, p):
                if has_norm(n):
                    load_ctx(sp, c, n + 2, p)
            over_items(sp, step1)

            def step3(n, p):
                if has_back(n):
                    sp.wait_ge(d["x"], n + 1)
                    sp.dma_start(out[n], acc[:, p, :]).then_inc(out_stored[p], 16)
            over_items(sp, step3)
            sp.wait_ge(out_stored[0], 8 * NB)
            sp.wait_ge(out_stored[1], 8 * NB)

        @block.gpsimd
        def _(pool):
            nc.gpsimd.memset(ident[:], 0.0).then_inc(pool_self, 1)
            nc.gpsimd.memset(sel[:], 0.0).then_inc(pool_self, 1)
            nc.gpsimd.memset(ones3[:], 1.0)
            nc.gpsimd.memset(one1[:], 1.0)
            nc.gpsimd.memset(expo[:], -0.5)
            nc.gpsimd.memset(mp[:], 0.0)
            nc.gpsimd.memset(V0[:, :, :, DH0:], 1.0)
            nc.gpsimd.memset(V1[:, :, :, DH1:], 1.0)
            nc.gpsimd.iota(iota8[:], [[1, NE]], base=0, channel_multiplier=0, allow_small_or_imprecise_dtypes=True)
            for k in range(3):
                nc.gpsimd.memset(patt[0:1, 4, k:k + 1], bf16_parts(FILL0)[k])
            nc.gpsimd.memset(patt[0:1, 4, 3:], 0.0)
            for k, low in ((0, (2, 3)), (1, (1, 3))):
                row = patt[0:1, 2 * k:2 * k + 2, :].rearrange("o k (j r d) -> o k j r d", j=G, r=REPS)
                for r in range(REPS):
                    nc.gpsimd.memset(row[:, 0, :, r, :], -1.0 if r in low else 1.0)
                    nc.gpsimd.memset(row[:, 1, :, r, :], 1.0 if r in low else 0.0)
            pool.wait_ge(pool_self, 2)
            nc.gpsimd.affine_select(out=ident[:], in_=ident[:], compare_op=ALU.not_equal, fill=1.0, base=0,
                                    pattern=[[-1, P]], channel_multiplier=1).then_inc(pool_self, 1)
            for k in range(3):
                nc.gpsimd.affine_select(out=sel[:, 0:NH, :], in_=sel[:, 0:NH, :], compare_op=ALU.not_equal, fill=1.0,
                                        base=-k * NH, pattern=[[-1, NH], [0, P]], channel_multiplier=1).then_inc(pool_self, 1)
                nc.gpsimd.affine_select(out=sel[:, NH, :], in_=sel[:, NH, :], compare_op=ALU.not_equal, fill=1.0,
                                        base=-3 * NH - k, pattern=[[0, P]], channel_multiplier=1).then_inc(pool_self, 1)
                pool.wait_ge(pool_self, 5 + 2 * k)
            nc.gpsimd.tensor_copy(identb[:], ident[:]).then_inc(const_ready, 1)
            nc.gpsimd.memset(QBD[:].rearrange("p a g j s -> p (a g j s)").bitcast(FP32), 0.0).then_inc(bd_zeroed, 1)

            norm_pool(pool, a, 0, 0)

            def step0(n, p):
                if has_norm(n):
                    norm_pool(pool, a, n + 2, p)
                if has_front(n):
                    max_parts_pool(pool, a, n + 1, 1 - p, False)
            over_items(pool, step0)

            def stepb(n, p):
                if has_norm(n):
                    norm_pool(pool, b, n + 2, p)
            norm_pool(pool, b, 0, 0)
            over_items(pool, stepb)

            def step1(n, p):
                if has_norm(n):
                    norm_pool(pool, c, n + 2, p)
                if has_front(n):
                    max_parts_pool(pool, c, n + 1, 1 - p, True)
            norm_pool(pool, c, 0, 0)
            over_items(pool, step1)

            def stepd(n, p):
                if has_norm(n):
                    norm_pool(pool, d, n + 2, p)
            norm_pool(pool, d, 0, 0)
            over_items(pool, stepd)

        @block.scalar
        def _(act):
            for t, src in ((gw[:], gate_w), (w1[:], moe_w1.rearrange("e d h -> d e h")),
                           (w2[:], moe_w2.rearrange("e (c p) d -> p e c d", p=P)), (f1[:], ffn_w1),
                           (f2[:], ffn_w2.rearrange("(c p) d -> p c d", p=P)), (fb1[:], ffn_b1.rearrange("(c p) -> p c", p=P))):
                act.dma_start(t, src).then_inc(ld_ffn, 16)
            for t, src in ((nat1[:, 0, :], wq1), (nat1[:, 1, :], wkv1[:, 0:INNER]), (wv1[:], wkv1[:, INNER:]),
                           (wout[:], wout1.rearrange("(c p) d -> p c d", p=P))):
                act.dma_start(t, src).then_inc(ld_w1, 16)

            def read_xct(s, m, p, both, free_sem, free_count):
                act.wait_ge(s["tr"], m + 1)
                wait(act, free_sem, free_count)
                k = 2 if both else 1
                nc.scalar.activation(XCT[:, p, 0:k, :], M_BANK[:, 0:k * P].rearrange("p (k s) -> p k s", k=k),
                                     ACT.Copy).then_inc(s["xct"], 1)

            def read_mT(s, m, p):
                act.wait_ge(s["mt"], m + 1)
                wait(act, s["t"], NU * (m - 1))
                nc.scalar.activation(MT[:, p, :], M_BANK[0:MROWS, 0:P // 2].bitcast(BF16), ACT.Copy).then_inc(s["mT"], 1)

            def probabilities(s, m, g, bias):
                u = NU * m + g
                wait_apart(act, (s["t"], u + 1), (s["pv"], u - 1))
                nc.scalar.activation(PR[:, g % 2, :], T_BANK[g % 2][:], ACT.Exp, bias=bias).then_inc(s["e"], 1)

            def step0(n, p):
                q = 1 - p
                if has_front(n):
                    read_xct(a, n + 1, q, True, a["t"], NU * n)
                if has_back(n):
                    read_mT(a, n, p)
                    for g in (0, 1):
                        probabilities(a, n, g, mk_col[:, bass.ds(n, 1)])
                if has_front(n):
                    act.wait_ge(a["v0"], n + 2)
                    wait(act, a["pv"], NU * n)
                    nc.scalar.activation(V0[:, q, :, 0:DH0], M_BANK[:, 0:P].rearrange("p (h d) -> p h d", h=NH),
                                         ACT.Copy).then_inc(a["vc"], 1)
                if has_back(n):
                    for g in (2, 3):
                        probabilities(a, n, g, mk_col[:, bass.ds(n, 1)])
                    act.wait_ge(a["ot"], n + 1)
                    wait(act, a["o"], n - 1)
                    nc.scalar.activation(OT[:, p, 0, :], M_BANK[:, 0:P], ACT.Copy).then_inc(a["oT"], 1)
            over_items(act, step0)

            def stepb(n, p):
                if has_front(n):
                    read_xct(b, n + 1, 1 - p, False, b["h"], NE * n)
                if has_back(n):
                    act.wait_ge(b["d"], n + 1)
                    nc.scalar.activation(gcol[:, p, 1:2], gcol[:, p, 0:1], ACT.Exp).then_inc(b["e"], 1)
                    for e in range(NE):
                        u = NE * n + e
                        act.wait_ge(b["h"], u + 1)
                        wait(act, b["y"], u - 1)
                        nc.scalar.activation(H[:, e % 2, :, :].rearrange("p c s -> p (c s)"), bank[e % 2][:],
                                             ACT.Relu).then_inc(b["hr"], 1)
            over_items(act, stepb)

            def step1(n, p):
                q = 1 - p
                front, back = has_front(n), has_back(n)

                def values(half):
                    u = 2 * (n + 1) + half
                    act.wait_ge(c["v"], u + 1)
                    wait(act, c["pv"], NU * n)
                    nc.scalar.activation(V1[:, q, 8 * half:8 * half + 8, 0:DH1],
                                         bank[4][:].rearrange("p (h d) -> p h d", h=8), ACT.Copy).then_inc(c["vc"], 1)

                def y_unit(g):
                    act.wait_ge(c["y"], NU * (n + 1) + g + 1)
                    wait(act, c["t"], NU * n)
                    nc.scalar.activation(YT[:, q, G * g:G * g + G, :].rearrange("p h s -> p (h s)"), bank[4][:],
                                         ACT.Copy).then_inc(c["yc"], 1)

                def heads_T(g):
                    u = NU * n + g
                    act.wait_ge(c["ot"], u + 1)
                    wait(act, c["o"], n - 1)
                    nc.scalar.activation(OT[:, p, 2 * g:2 * g + 2, :].rearrange("p c s -> p (c s)"), M_BANK[:, 0:2 * P],
                                         ACT.Copy).then_inc(c["oT"], 1)

                if front:
                    read_xct(c, n + 1, q, True, c["t"], NU * n)
                if back:
                    read_mT(c, n, p)
                    probabilities(c, n, 0, 0.0)
                if front:
                    values(0)
                if back:
                    probabilities(c, n, 1, 0.0)
                if front:
                    values(1)
                    y_unit(0)
                if back:
                    probabilities(c, n, 2, 0.0)
                if front:
                    y_unit(1)
                if back:
                    heads_T(0)
                    probabilities(c, n, 3, 0.0)
                if front:
                    y_unit(2)
                if back:
                    heads_T(1)
                if front:
                    y_unit(3)
                if back:
                    heads_T(2)
                    heads_T(3)
            over_items(act, step1)

            def stepd(n, p):
                if has_front(n):
                    read_xct(d, n + 1, 1 - p, False, d["h"], n)
                if has_back(n):
                    act.wait_ge(d["h"], n + 1)
                    wait(act, d["y"], n - 1)
                    for k in range(HC):
                        last = nc.scalar.activation(H[:, p, k, :], bank[p][:, k * P:(k + 1) * P], ACT.Relu, bias=fb1[:, k:k + 1])
                    last.then_inc(d["hr"], 1)
            over_items(act, stepd)

        @block.vector
        def _(dve):
            chain = [0]

            def link(ins):
                chain[0] += 1
                ins.then_inc(dve_self, 1)
                dve.wait_ge(dve_self, chain[0])

            dve.wait_ge(ld_setup, 16 * (2 + 4 + 2 * G * REPS + 2))
            link(nc.vector.tensor_scalar(mk_f[:, 0, :], mk_u8[:], -1.0, None, ALU.add))
            link(nc.vector.tensor_scalar(mk_f[:, 1, :], mk_f[:, 0, :], FILL0, None, ALU.mult))
            link(nc.vector.tensor_scalar(mq_f[:, 0, :], mq_i[:], -1.0, 1.0, ALU.mult, ALU.add))
            nc.vector.tensor_scalar(mq_f[:, 1, :], mq_f[:, 0, :], FILL1, None, ALU.mult).then_inc(parts_ready, 1)
            link(nc.vector.tensor_copy(brow_b[:, :, 0, :], brow_f[:, 0:4, 0, :]))
            link(nc.vector.tensor_tensor(brow_f[:, 0:4, 1, :], brow_f[:, 0:4, 0, :], brow_b[:, :, 0, :], ALU.subtract))
            link(nc.vector.tensor_copy(brow_b[:, :, 1, :], brow_f[:, 0:4, 1, :]))
            nc.vector.tensor_tensor(brow_b[:, :, 2, :], brow_f[:, 0:4, 1, :], brow_b[:, :, 1, :],
                                    ALU.subtract).then_inc(parts_ready, 1)
            dve.wait_ge(set_pe, 1)
            nc.vector.tensor_copy(mk_col[:], bank[0][:, 0:NB])
            link(nc.vector.tensor_copy(c_col[:], bank[0][:, NB:2 * NB]))
            link(nc.vector.tensor_copy(pcol[:], bank[0][:, 2 * NB:2 * NB + 5]))
            nc.vector.tensor_scalar(mk_rows[:], mk3[:], -1.0, pcol[0:3, 4:5], ALU.add, ALU.mult)
            link(nc.vector.tensor_scalar(c_tmp[:, 0, :], c_col[:], -1.0, None, ALU.mult))
            link(nc.vector.tensor_copy(c_parts[:, :, 0], c_tmp[:, 0, :]))
            link(nc.vector.tensor_tensor(c_tmp[:, 1, :], c_tmp[:, 0, :], c_parts[:, :, 0], ALU.subtract))
            link(nc.vector.tensor_copy(c_parts[:, :, 1], c_tmp[:, 1, :]))
            link(nc.vector.tensor_tensor(c_parts[:, :, 2], c_tmp[:, 1, :], c_parts[:, :, 1], ALU.subtract))
            dve.wait_ge(set_pe, 2)
            for i in range(2):
                src = bank[1][:, i * P:(i + 1) * P].rearrange("p (g j d) -> p g j d", g=NU, j=G)
                dst = wqk_rep[:, i, :, :].rearrange("p g (j r d) -> p g j r d", j=G, r=REPS)
                for r in range(REPS):
                    for g in range(NU):
                        nc.vector.tensor_copy(dst[:, g, :, r, :], src[:, g, :, :])
            nc.vector.tensor_copy(wv0T[:], bank[1][:, 2 * P:3 * P])
            nc.vector.tensor_copy(wo0T[:], bank[1][:, 3 * P:4 * P])
            link(nc.vector.tensor_scalar(bqk[:, 0, :], bqk[:, 0, :], float(DH0) ** -0.5, None, ALU.mult))
            nc.vector.memset(mpf[:, 2, 0:1], 0.0).then_inc(set_copy, 1)
            for t in range(2 * PAIRS // 4):
                dve.wait_ge(set_pe, 3 + t)
                i, k = t // 2, 4 * (t % 2)
                nc.vector.tensor_copy(qkT[:, i, k:k + 4, :].rearrange("p c s -> p (c s)"), bank[2 + t % 2][:]).then_inc(set_copy, 1)
            for g in range(NU):
                dve.wait_ge(set_pe, 7 + g)
                even_odd = A[:, 8 * (g // 2):8 * (g // 2) + 8, :].rearrange("p (j o) s -> p o j s", o=2)
                nc.vector.tensor_scalar(even_odd[:, g % 2], bank[2 + g % 2][:].rearrange("p (j s) -> p j s", j=G),
                                        float(DH1) ** -0.5, None, ALU.mult).then_inc(set_copy, 1)
            SETUP_COPIES = 1 + 4 + NU
            dve.wait_ge(set_copy, SETUP_COPIES)
            dve.wait_ge(ld_x, 64)

            def row_max(s, m, p, g):
                u = NU * m + g
                dve.wait_ge(s["s"], u + 1)
                wait(dve, s["mp"], m - 1)
                nc.vector.tensor_reduce(mx[:, p, G * g:G * g + G], S_BANK[g % 2][:].rearrange("p (j k) -> p j k", j=G),
                                        AXX, ALU.max).then_inc(s["mx"], 1)

            norm_dve_stats(dve, a, None, 0, 0)
            norm_dve_apply(dve, a, 0, 0)

            def step0(n, p):
                q = 1 - p
                if has_norm(n):
                    norm_dve_stats(dve, a, None, n + 2, p)
                if has_front(n):
                    m = n + 1
                    dve.wait_ge(a["q"], m + 1)
                    for g in range(NU):
                        last = nc.vector.tensor_scalar(QF[:, 0, g, :], bank[4][:, g * P:(g + 1) * P], float(DH0) ** -0.5,
                                                       bqk[:, 0, g:g + 1], ALU.mult, ALU.add)
                    last.then_inc(a["qf"], 1)
                    dve.wait_ge(a["k"], m + 1)
                    for g in range(NU):
                        last = nc.vector.scalar_tensor_tensor(QF[:, 1, g, :], bank[5][:, g * P:(g + 1) * P],
                                                              bqk[:, 1, g:g + 1], mk_bc[:, bass.ds(m * P, P)],
                                                              ALU.add, ALU.mult)
                    last.then_inc(a["kf"], 1)
                    for i, done in ((0, "qf"), (1, "kf")):
                        dve.wait_ge(a[done], m + 1)
                        nc.vector.tensor_scalar(HF[:, i, :, :].bitcast(FP32R), QF[:, i, :, :], pcol[:, 2 * i:2 * i + 1], None,
                                                ALU.mult).then_inc(a["hf"], 1)
                    dve.wait_ge(a["hf"], 2 * m + 1)
                    wait(dve, a["bd"], 16 * G * m)
                    nc.vector.scalar_tensor_tensor(QS[:], QF[:, 0, :, :], pcol[:, 1:2], HF[:, 0, :, :],
                                                   ALU.mult, ALU.add).then_inc(a["qs"], 1)
                    dve.wait_ge(a["hf"], 2 * m + 2)
                    wait(dve, a["t"], NU * n)
                    nc.vector.scalar_tensor_tensor(KS[:, q, :, :], QF[:, 1, :, :], pcol[:, 3:4], HF[:, 1, :, :],
                                                   ALU.mult, ALU.add).then_inc(a["ks"], 1)
                if has_norm(n):
                    norm_dve_apply(dve, a, n + 2, p)
                if has_front(n):
                    for g in (0, 1):
                        row_max(a, n + 1, q, g)
                if has_back(n):
                    dve.wait_ge(a["pv"], NU * (n + 1))
                    o = bank[6][:, 0:NH * (DH0 + 1)].rearrange("p (h d) -> p h d", h=NH)
                    nc.vector.reciprocal(rden[:, p, :], o[:, :, DH0]).then_inc(a["rd"], 1)
                    dve.wait_ge(a["rd"], n + 1)
                    wait(dve, a["ot"], n - 1)
                    nc.vector.tensor_tensor(ON[:, p, 0:P].rearrange("p (h d) -> p h d", h=NH), o[:, :, 0:DH0],
                                            rden[:, p, :].unsqueeze(2).broadcast_to([P, NH, DH0]),
                                            ALU.mult).then_inc(a["on"], 1)
                if has_front(n):
                    for g in (2, 3):
                        row_max(a, n + 1, q, g)
                if has_back(n):
                    dve.wait_ge(a["o"], n + 1)
                    nc.vector.tensor_tensor(X[:, bass.ds(n, 1), :].rearrange("p o d -> p (o d)"), M_BANK[:, 0:P],
                                            X[:, bass.ds(n, 1), :].rearrange("p o d -> p (o d)"),
                                            ALU.add).then_inc(a["x"], 1)
            over_items(dve, step0)

            norm_dve_stats(dve, b, a["x"], 0, 0)
            norm_dve_apply(dve, b, 0, 0)

            def stepb(n, p):
                if has_norm(n):
                    norm_dve_stats(dve, b, a["x"], n + 2, p)
                    norm_dve_apply(dve, b, n + 2, p)
                if has_back(n):
                    dve.wait_ge(b["lg"], n + 1)
                    nc.vector.tensor_copy(lg[:, p, :], bank[6][:, 0:NE]).then_inc(b["lgc"], 1)
                    wait_apart(dve, (b["lgc"], n + 1))
                    nc.vector.max(top[:, p, :], lg[:, p, :]).then_inc(b["top"], 1)
                    dve.wait_ge(b["top"], n + 1)
                    nc.vector.tensor_tensor(gcol[:, p, 0:1], top[:, p, 1:2], top[:, p, 0:1], ALU.subtract).then_inc(b["d"], 1)
                    nc.vector.max_index(topi[:, p, :], top[:, p, :], lg[:, p, :]).then_inc(b["topi"], 1)
                    dve.wait_ge(b["topi"], n + 1)
                    nc.vector.tensor_copy(topf[:, p, :], topi[:, p, 0:2]).then_inc(b["topf"], 1)
                    dve.wait_ge(b["e"], n + 1)
                    nc.vector.tensor_scalar(gcol[:, p, 2:3], gcol[:, p, 1:2], 1.0, None, ALU.add).then_inc(b["g"], 1)
                    dve.wait_ge(b["g"], 3 * n + 1)
                    nc.vector.reciprocal(gcol[:, p, 3:4], gcol[:, p, 2:3]).then_inc(b["g"], 1)
                    dve.wait_ge(b["g"], 3 * n + 2)
                    nc.vector.tensor_tensor(gcol[:, p, 4:5], gcol[:, p, 3:4], gcol[:, p, 1:2], ALU.mult).then_inc(b["g"], 1)
                    dve.wait_ge(b["topf"], n + 1)
                    dve.wait_ge(b["g"], 3 * n + 3)
                    for k in range(2):
                        last = nc.vector.tensor_scalar(comb[:, p, k, :], iota8[:], topf[:, p, k:k + 1], gcol[:, p, 3 + k:4 + k],
                                                       ALU.is_equal, ALU.mult)
                    last.then_inc(b["comb"], 1)
                    dve.wait_ge(b["comb"], 2 * n + 1)
                    nc.vector.tensor_tensor(comb[:, p, 0, :], comb[:, p, 0, :], comb[:, p, 1, :], ALU.add).then_inc(b["comb"], 1)
                    dve.wait_ge(b["comb"], 2 * n + 2)
                    xrow = X[:, bass.ds(n, 1), :].rearrange("p o d -> p (o d)")
                    for e in range(NE):
                        u = NE * n + e
                        dve.wait_ge(b["y"], u + 1)
                        if e:
                            dve.wait_ge(b["yacc"], u)
                        nc.vector.scalar_tensor_tensor(xrow if e == NE - 1 else acc[:, e % 2, :], bank[4 + e % 2][:, 0:P],
                                                       comb[:, p, 0, e:e + 1], acc[:, (e + 1) % 2, :] if e else xrow,
                                                       ALU.mult, ALU.add).then_inc(b["yacc"], 1)
            over_items(dve, stepb)

            norm_dve_stats(dve, c, None, 0, 0)
            norm_dve_apply(dve, c, 0, 0)

            def step1(n, p):
                q = 1 - p
                front, back = has_front(n), has_back(n)

                def normalise(g):
                    u = NU * n + g
                    dve.wait_ge(c["pv"], u + 1)
                    o = bank[5 + g % 2][:, 0:G * (DH1 + 1)].rearrange("p (h d) -> p h d", h=G)
                    nc.vector.reciprocal(rden[:, p, G * g:G * g + G], o[:, :, DH1]).then_inc(c["rd"], 1)
                    dve.wait_ge(c["rd"], u + 1)
                    wait(dve, c["ot"], u - 1)
                    nc.vector.tensor_tensor(ON[:, g % 2, :].rearrange("p (h d) -> p h d", h=G), o[:, :, 0:DH1],
                                            rden[:, p, G * g:G * g + G].unsqueeze(2).broadcast_to([P, G, DH1]),
                                            ALU.mult).then_inc(c["on"], 1)

                if has_norm(n):
                    norm_dve_stats(dve, c, None, n + 2, p)
                if back:
                    normalise(0)
                    normalise(1)
                if has_norm(n):
                    norm_dve_apply(dve, c, n + 2, p)
                if front:
                    row_max(c, n + 1, q, 0)
                if back:
                    normalise(2)
                if front:
                    row_max(c, n + 1, q, 1)
                if back:
                    normalise(3)
                if front:
                    row_max(c, n + 1, q, 2)
                    row_max(c, n + 1, q, 3)
                if back:
                    dve.wait_ge(c["o"], n + 1)
                    xrow = X[:, bass.ds(n, 1), :].rearrange("p o d -> p (o d)")
                    nc.vector.tensor_tensor(xrow, M_BANK[:, 0:P], xrow, ALU.add).then_inc(c["x"], 1)
            over_items(dve, step1)

            norm_dve_stats(dve, d, c["x"], 0, 0)
            norm_dve_apply(dve, d, 0, 0)

            def stepd(n, p):
                if has_norm(n):
                    norm_dve_stats(dve, d, c["x"], n + 2, p)
                    norm_dve_apply(dve, d, n + 2, p)
                if has_back(n):
                    dve.wait_ge(d["y"], n + 1)
                    wait(dve, out_stored[p], loads(n - 2, p))
                    nc.vector.tensor_tensor(acc[:, p, :], bank[4 + p][:, 0:P],
                                            X[:, bass.ds(n, 1), :].rearrange("p o d -> p (o d)"),
                                            ALU.add).then_inc(d["x"], 1)
            over_items(dve, stepd)

        @block.tensor
        def _(pe):
            mm = nc.tensor.matmul
            pe.wait_ge(const_ready, 1)
            pe.wait_ge(parts_ready, 1)
            nc.tensor.transpose(bank[0][:, 0:NB], mk_f[:, 1, :], ident[0:NB, 0:NB])
            nc.tensor.transpose(bank[0][:, NB:2 * NB], mq_f[:, 1, :], ident[0:NB, 0:NB])
            for k in range(5):
                last = mm(bank[0][:, 2 * NB + k:2 * NB + k + 1], patt[0:1, k, :], one1[:], start=True, stop=True)
            last.then_inc(set_pe, 1)
            pe.wait_ge(ld_w0, 64)
            for i in range(4):
                last = nc.tensor.transpose(bank[1][:, i * P:(i + 1) * P], nat0[:, i, :], ident[:])
            last.then_inc(set_pe, 1)
            pe.wait_ge(ld_w1, 64)
            for t in range(2 * PAIRS // 4):
                i, k = t // 2, 4 * (t % 2)
                if t >= 2:
                    pe.wait_ge(set_copy, 1 + t - 1)
                for j in range(4):
                    last = nc.tensor.transpose(bank[2 + t % 2][:, j * P:(j + 1) * P], nat1[:, i, (k + j) * P:(k + j + 1) * P], ident[:])
                last.then_inc(set_pe, 1)
            for g in range(NU):
                pe.wait_ge(set_copy, 1 + 4 + max(0, g - 1))
                for j in range(G):
                    h = 8 * (g // 2) + 2 * j + g % 2
                    rows = slice(DH1 * (h % 2), DH1 * (h % 2 + 1))
                    last = mm(bank[2 + g % 2][:, j * P:(j + 1) * P], qkT[rows, 0, h // 2, :], qkT[rows, 1, h // 2, :],
                              start=True, stop=True)
                last.then_inc(set_pe, 1)
            pe.wait_ge(set_copy, 1 + 4 + NU)
            pe.wait_ge(rows_moved, 48)

            def transpose_in(s, m, p, both, m_free, m_count):
                pe.wait_ge(s["xn"], m + 1)
                if both:
                    pe.wait_ge(s[f"ctx{p}"], loads(m, p))
                wait(pe, m_free, m_count)
                last = nc.tensor.transpose(M_BANK[:, 0:P], XN[:, p, :], ident[:])
                if both:
                    last = nc.tensor.transpose(M_BANK[:, P:2 * P], CX[:, p, :], ident[:])
                last.then_inc(s["tr"], 1)

            def transpose_max(s, m, p, m_free, m_count):
                wait_apart(pe, (s["mp"], m + 1), (m_free, m_count))
                nc.tensor.transpose(M_BANK[0:MROWS, 0:P // 2].bitcast(BF16), mp[:, p, :], identb[:]).then_inc(s["mt"], 1)

            def step0(n, p):
                q, m = 1 - p, n + 1
                front, back = has_front(n), has_back(n)

                def scores_T(g):
                    u = NU * n + g
                    wait(pe, a["e"], u - 1)
                    mm(T_BANK[g % 2][:], KS[:, p, g, :], QBD[:, p, g, :, :].rearrange("p j s -> p (j s)"),
                       start=True, stop=False, skip_group_check=True)
                    add_minus_max(a, n, p, g, a["t"], T_BANK[g % 2])

                def values(g):
                    pe.wait_ge(a["e"], NU * n + g + 1)
                    if g == 0:
                        pe.wait_ge(a["vc"], n + 1)
                        wait(pe, a["on"], n)
                    for j in range(G):
                        h = G * g + j
                        last = mm(bank[6][:, h * (DH0 + 1):(h + 1) * (DH0 + 1)], PR[:, g % 2, j * P:(j + 1) * P],
                                  V0[:, p, h, :], start=True, stop=True)
                    last.then_inc(a["pv"], 1)

                if front:
                    if isinstance(n, int) and n == 0:
                        pe.wait_ge(a["vc"], 1)
                    transpose_in(a, m, q, True, a["x"], n)
                if back:
                    transpose_max(a, n, p, *((a["xct"], n + 2) if front else (a["x"], n)))
                if front:
                    pe.wait_ge(a["xct"], m + 1)
                    for i, name, done in ((0, "q", "qf"), (1, "k", "kf")):
                        wait(pe, a[done], m)
                        for g in range(NU):
                            last = mm(bank[4 + i][:, g * P:(g + 1) * P], wqk_rep[:, i, g, :], XCT[:, q, i, :], start=True, stop=True)
                        last.then_inc(a[name], 1)
                if back:
                    pe.wait_ge(a["mT"], n + 1)
                    scores_T(0)
                    scores_T(1)
                if front:
                    wait(pe, a["mT"], m)
                    mm(M_BANK[:, 0:P], XCT[:, q, 1, :], wv0T[:], start=True, stop=False)
                    mm(M_BANK[:, 0:P], ones3[:], brow[:, 0, :], start=False, stop=True).then_inc(a["v0"], 1)
                if back:
                    values(0)
                    scores_T(2)
                    values(1)
                    scores_T(3)

                def scores(g):
                    u = NU * m + g
                    wait_apart(pe, (a["mx"], u - 1))
                    if g == 0:
                        pe.wait_ge(a["ks"], m + 1)
                        pe.wait_ge(a["bd"], 16 * G * (m + 1))
                    mm(S_BANK[g % 2][:].rearrange("p (j k) -> p j k", j=G), ones3[:],
                       mk_rows[:, bass.ds(m * P, P)].unsqueeze(1).broadcast_to([3, G, P]), start=True, stop=False,
                       skip_group_check=True)
                    for j in range(G):
                        last = mm(S_BANK[g % 2][:, j * P:(j + 1) * P], QBD[:, q, g, j, :], KS[:, q, g, :],
                                  start=False, stop=(j == G - 1), skip_group_check=True)
                    last.then_inc(a["s"], 1)

                if front:
                    scores(0)
                if back:
                    values(2)
                if front:
                    scores(1)
                if back:
                    values(3)
                if front:
                    scores(2)
                if back:
                    pe.wait_ge(a["on"], n + 1)
                    wait(pe, a["vc"], min(n + 2, NB) if isinstance(n, int) else n + 2)
                    nc.tensor.transpose(M_BANK[:, 0:P], ON[:, p, 0:P], ident[:]).then_inc(a["ot"], 1)
                if front:
                    scores(3)
                if back:
                    pe.wait_ge(a["oT"], n + 1)
                    mm(M_BANK[:, 0:P], OT[:, p, 0, :], wo0T[:], start=True, stop=False)
                    mm(M_BANK[:, 0:P], ones3[:], brow[:, 1, :], start=False, stop=True).then_inc(a["o"], 1)
            over_items(pe, step0)

            pe.wait_ge(ld_ffn, 96)

            def stepb(n, p):
                if has_front(n):
                    transpose_in(b, n + 1, 1 - p, False, b["xct"] if not is_start(n) else a["x"], n + 1 if not is_start(n) else NB)
                if has_back(n):
                    pe.wait_ge(b["xct"], n + 1)
                    wait(pe, b["lgc"], n)
                    mm(bank[6][:, 0:NE], XCT[:, p, 0, :], gw[:], start=True, stop=True).then_inc(b["lg"], 1)

                    def hidden(e):
                        wait(pe, b["hr"], NE * n + e - 1)
                        for k in range(HC):
                            last = mm(bank[e % 2][:, k * P:(k + 1) * P], w1[:, e, k * P:(k + 1) * P], XCT[:, p, 0, :],
                                      start=True, stop=True)
                        last.then_inc(b["h"], 1)

                    hidden(0)
                    for e in range(NE):
                        if e + 1 < NE:
                            hidden(e + 1)
                        pe.wait_ge(b["hr"], NE * n + e + 1)
                        wait(pe, b["yacc"], NE * n + e - 1)
                        for k in range(HC):
                            last = mm(bank[4 + e % 2][:, 0:P], H[:, e % 2, k, :], w2[:, e, k, :], start=(k == 0), stop=(k == HC - 1))
                        last.then_inc(b["y"], 1)
            over_items(pe, stepb)

            def step1(n, p):
                q, m = 1 - p, n + 1
                front, back = has_front(n), has_back(n)

                def project_v(half):
                    wait(pe, c["yc"], NU * m) if half == 0 else wait(pe, c["vc"], 2 * m + 1)
                    mm(bank[4][:], XCT[:, q, 1, :], wv1[:, 512 * half:512 * half + 512], start=True, stop=True).then_inc(c["v"], 1)

                def project_y(g):
                    if g == 0:
                        pe.wait_ge(c["vc"], 2 * m + 2)
                    else:
                        pe.wait_ge(c["yc"], NU * m + g)
                    for j in range(G):
                        last = mm(bank[4][:, j * P:(j + 1) * P], A[:, G * g + j, :], XCT[:, q, 0, :], start=True, stop=True)
                    last.then_inc(c["y"], 1)

                def scores(g):
                    u = NU * m + g
                    pe.wait_ge(c["yc"], u + 1)
                    wait(pe, c["mx"], u - 1)
                    for j in range(G):
                        last = mm(S_BANK[g % 2][:, j * P:(j + 1) * P], YT[:, q, G * g + j, :], XCT[:, q, 1, :], start=True, stop=True)
                    last.then_inc(c["s"], 1)

                def scores_T(g):
                    u = NU * n + g
                    wait(pe, c["e"], u - 1)
                    t = T_BANK[g % 2]
                    mm(t[:], XCT[:, p, 1, :], YT[:, p, G * g:G * g + G, :].rearrange("p h s -> p (h s)"),
                       start=True, stop=False, skip_group_check=True)
                    mm(t[:].rearrange("p (j s) -> p j s", j=G), sel[:, NH, :],
                       MT[:, p, :].unsqueeze(1).broadcast_to([MROWS, G, P]), start=False, stop=False, skip_group_check=True)
                    add_minus_max(c, n, p, g, c["t"], t)

                def values(g):
                    u = NU * n + g
                    pe.wait_ge(c["e"], u + 1)
                    wait(pe, c["on"], u - 1)
                    for j in range(G):
                        last = mm(bank[5 + g % 2][:, j * (DH1 + 1):(j + 1) * (DH1 + 1)], PR[:, g % 2, j * P:(j + 1) * P],
                                  V1[:, p, G * g + j, :], start=True, stop=True)
                    last.then_inc(c["pv"], 1)

                def transpose_heads(g):
                    u = NU * n + g
                    pe.wait_ge(c["on"], u + 1)
                    if g == 0:
                        pe.wait_ge(c["mT"], n + 1)
                    else:
                        pe.wait_ge(c["oT"], u)
                    for k in range(2):
                        last = nc.tensor.transpose(M_BANK[:, k * P:(k + 1) * P], ON[:, g % 2, k * P:(k + 1) * P], ident[:])
                    last.then_inc(c["ot"], 1)

                if front:
                    if is_start(n):
                        pe.wait_ge(b["yacc"], NE * NB)
                    transpose_in(c, m, q, True, c["x"] if not is_start(n) else b["xct"], n if not is_start(n) else NB)
                if back:
                    transpose_max(c, n, p, *((c["xct"], n + 2) if front else (c["x"], n)))
                    pe.wait_ge(c["mT"], n + 1)
                    scores_T(0)
                if front:
                    pe.wait_ge(c["xct"], m + 1)
                    project_v(0)
                if back:
                    scores_T(1)
                if front:
                    project_v(1)
                if back:
                    values(0)
                if front:
                    project_y(0)
                if back:
                    scores_T(2)
                    values(1)
                if front:
                    project_y(1)
                    scores(0)
                if back:
                    transpose_heads(0)
                    scores_T(3)
                    values(2)
                if front:
                    project_y(2)
                    scores(1)
                if back:
                    transpose_heads(1)
                    values(3)
                if front:
                    project_y(3)
                    scores(2)
                if back:
                    transpose_heads(2)
                if front:
                    scores(3)
                if back:
                    transpose_heads(3)
                    pe.wait_ge(c["oT"], NU * (n + 1))
                    for k in range(PAIRS):
                        mm(M_BANK[:, 0:P], OT[:, p, k, :], wout[:, k, :], start=(k == 0), stop=False)
                    mm(M_BANK[:, 0:P], ones3[:], brow[:, 2, :], start=False, stop=True).then_inc(c["o"], 1)
            over_items(pe, step1)

            def stepd(n, p):
                if has_front(n):
                    transpose_in(d, n + 1, 1 - p, False, d["xct"] if not is_start(n) else c["x"], n + 1 if not is_start(n) else NB)
                if has_back(n):
                    pe.wait_ge(d["xct"], n + 1)
                    wait(pe, d["hr"], n - 1)
                    for k in range(HC):
                        last = mm(bank[p][:, k * P:(k + 1) * P], f1[:, k * P:(k + 1) * P], XCT[:, p, 0, :], start=True, stop=True)
                    last.then_inc(d["h"], 1)
                    pe.wait_ge(d["hr"], n + 1)
                    wait(pe, d["x"], n - 1)
                    for k in range(HC):
                        mm(bank[4 + p][:, 0:P], H[:, p, k, :], f2[:, k, :], start=(k == 0), stop=False)
                    mm(bank[4 + p][:, 0:P], ones3[:], brow[:, 3, :], start=False, stop=True).then_inc(d["y"], 1)
            over_items(pe, stepd)


_INS = ["x", "ctx_1024", "mask_BxS2_bf1", "mask_BxS_ik0", "L0_xattn_Wq", "L0_xattn_bq", "L0_xattn_Wk", "L0_xattn_bk",
        "L0_xattn_Wv", "L0_xattn_bv", "L0_xattn_Wo", "L0_xattn_bo", "L0_ffn_w_gate", "L0_ffn_w1", "L0_ffn_w2",
        "L1_xattn_Wq", "L1_xattn_Wkv", "L1_xattn_Wout", "L1_xattn_bout", "L1_ffn_w1", "L1_ffn_b1", "L1_ffn_w2", "L1_ffn_b2"]


def kernel(**inputs):
    import numpy as _np
    import concourse.bacc as _bacc
    from concourse.bass_utils import run_bass_kernel_spmd as _run

    nc = _bacc.Bacc("TRN2", target_bir_lowering=False, num_devices=1)
    arrays, args = {}, []
    for name in _INS:
        a = _np.ascontiguousarray(inputs[name])
        arrays[f"in_{name}_dram"] = a
        args.append(nc.dram_tensor(f"in_{name}_dram", a.shape, mybir.dt.from_np(a.dtype), kind="ExternalInput").ap())
    args.append(nc.dram_tensor("out_0_dram", (NB, P, P), FP32, kind="ExternalOutput").ap())
    build(nc, *args)
    r = _run(nc, [arrays], core_ids=[0])
    return r.results[0]["out_0_dram"]
```

```python
import concourse.bass as bass
from concourse import mybir
from contextlib import ExitStack

FP32 = mybir.dt.float32
FP32R = mybir.dt.float32r
BF16 = mybir.dt.bfloat16
U8 = mybir.dt.uint8
U32 = mybir.dt.uint32
I32 = mybir.dt.int32
ALU = mybir.AluOpType
ACT = mybir.ActivationFunctionType
AXX = mybir.AxisListType.X

NB = 32
P = 128
NH = 16
G = 4
NU = NH // G
DH0 = P // NH
DH1 = 64
INNER = NH * DH1
PAIRS = INNER // P
NE = 8
HC = 4
REPS = 4
EPS = 1e-5
FILL0 = 1e8
FILL1 = 1e6


def bf16_parts(value):
    import numpy as np
    parts, rest = [], np.float32(value)
    for _ in range(3):
        bits = np.array([rest], np.float32).view(np.uint32)
        part = ((bits + 0x7FFF + ((bits >> 16) & 1)) & 0xFFFF0000).astype(np.uint32).view(np.float32)[0]
        parts.append(float(part))
        rest = np.float32(rest - part)
    return parts


def over_items(engine, step):
    for n in (-1, 0, 1):
        step(n, n % 2)
    with engine.Fori(1, NB // 2 - 1) as i:
        step(i * 2, 0)
        step(i * 2 + 1, 1)
    for n in (NB - 2, NB - 1):
        step(n, n % 2)


def over_steps(engine, step, first, last, ahead):
    loop_end = (NB - 1 - ahead) // 2
    for n in range(first, 2):
        step(n, n % 2)
    with engine.Fori(1, loop_end) as i:
        step(i * 2, 0)
        step(i * 2 + 1, 1)
    for n in range(2 * loop_end, last + 1):
        step(n, n % 2)


def exists(m):
    return not isinstance(m, int) or 0 <= m < NB


def loads(m, p):
    return 8 * (m - p) + 16


def has_front(n):
    return not (isinstance(n, int) and n + 1 >= NB)


def has_back(n):
    return not (isinstance(n, int) and n < 0)


def is_first(n):
    return isinstance(n, int) and n == -1


def is_start(n):
    return isinstance(n, int) and n == -1


def has_norm(n):
    return not (isinstance(n, int) and n + 2 >= NB)


def wait(engine, semaphore, value):
    if isinstance(value, int) and value <= 0:
        return
    engine.wait_ge(semaphore, value)


def build(nc, x, ctx_in, mask_keys, mask_queries, wq0, bq0, wk0, bk0, wv0, bv0, wo0, bo0,
          gate_w, moe_w1, moe_w2, wq1, wkv1, wout1, bout1, ffn_w1, ffn_b1, ffn_w2, ffn_b2, out, c_dram):
    ctx = ExitStack()
    with ctx:
        def sb(name, shape, dt=FP32):
            return ctx.enter_context(nc.sbuf_tensor(name, shape, dt))

        def sem(name):
            return ctx.enter_context(nc.semaphore(name))

        ctx.enter_context(nc.allow_non_contiguous_dma(reason="small bias and weight layouts"))
        bank = [ctx.enter_context(nc.psum_tensor(f"bank{i}", [P, 512], FP32)) for i in range(8)]
        S_BANK, T_BANK = bank[0:2], bank[2:4]
        M_BANK, M2_BANK = bank[7], bank[5]

        ident = sb("ident", [P, P])
        identb = sb("identb", [P, P], BF16)
        ones3 = sb("ones3", [3, P], BF16)
        one1 = sb("one1", [1, 1])
        ones_row = sb("ones_row", [3, 512], BF16)
        expo = sb("expo", [P, 1])
        iota8 = sb("iota8", [P, NE])
        X = sb("X", [P, NB, P])
        nat0 = sb("nat0", [P, 4, P])
        wqk_rep = sb("wqk_rep", [P, 2, NU, P])
        wv0T = sb("wv0T", [P, P])
        wo0T = sb("wo0T", [P, P])
        bqk = sb("bqk", [P, 2, NU])
        patt = sb("patt", [1, 5, P])
        pcol = sb("pcol", [P, 5])
        brow_f = sb("brow_f", [1, 5, 3, P])
        brow_b = sb("brow_b", [1, 4, 3, P], BF16)
        brow = sb("brow", [3, 4, P], BF16)
        mk_bc = sb("mk_bc", [P, NB * P], U8)
        mk3 = sb("mk3", [3, NB * P], U8)
        mk_rows = sb("mk_rows", [3, NB * P], BF16)
        mq_i = sb("mq_i", [NB, P], I32)
        mq_f = sb("mq_f", [NB, 3, P])
        mq_b = sb("mq_b", [NB, 3, P], BF16)
        c_rows = sb("c_rows", [3, NB * P], BF16)
        YT = sb("YT", [P, 2, NH, P])
        VZ = YT
        nat1 = YT[:, 0, :, :].rearrange("p (i k) s -> p i (k s)", i=2)
        qkT = YT[:, 1, :, :].rearrange("p (i k) s -> p i k s", i=2)
        A = sb("A", [P, NH, P])
        wv1 = sb("wv1", [P, INNER])
        wout = sb("wout", [P, PAIRS, P])
        gw = sb("gw", [P, NE])
        w1 = sb("w1", [P, NE, HC * P])
        w2 = sb("w2", [P, NE, HC, P])
        f1 = sb("f1", [P, HC * P])
        f2 = sb("f2", [P, HC, P])
        fb1 = sb("fb1", [P, HC])
        stats = sb("stats", [P, 3, 6])
        mv = sb("mv", [P, 3, 2])
        veps = sb("veps", [P, 3, 1])
        rstd = sb("rstd", [P, 3, 1])
        XN = sb("XN", [P, 2, P])
        CX = sb("CX", [P, 2, P])
        XCT = sb("XCT", [P, 2, 2, P])
        QF = sb("QF", [P, 2, NU, P])
        HF = sb("HF", [P, 2, NU, P])
        QS = sb("QS", [P, 2, NU, P], FP32R)
        KS = sb("KS", [P, NU, P], FP32R)
        KBD = sb("KBD", [P, 2, NU, G, P], FP32R)
        V1 = sb("V1", [P, 2, NH, DH1])
        nmx = sb("nmx", [P, 2, NH])
        den = sb("den", [P, 2, NH])
        rden = sb("rden", [P, 2, NH])
        PR = sb("PR", [P, NU, G * P])
        PT = sb("PT", [P, 2, G * P])
        OT = sb("OT", [P, 2, PAIRS, P])
        XND = sb("XND", [P, P])
        XDT = sb("XDT", [P, P])
        H = sb("H", [P, 2, HC, P])
        lg = sb("lg", [P, 2, NE])
        top = sb("top", [P, 2, 8])
        topi = sb("topi", [P, 2, 8], U32)
        topf = sb("topf", [P, 2, 2])
        gcol = sb("gcol", [P, 2, 5])
        comb = sb("comb", [P, 2, 2, NE])
        acc = sb("acc", [P, 2, P])

        ld_setup, ld_w0, ld_w1, ld_ffn, ld_x = (sem(s) for s in ("ld_setup", "ld_w0", "ld_w1", "ld_ffn", "ld_x"))
        const_ready, pool_self, dve_self, act_self = (sem(s) for s in ("const_ready", "pool_self", "dve_self", "act_self"))
        set_pe, set_copy, rows_moved, bd_zeroed = (sem(s) for s in ("set_pe", "set_copy", "rows_moved", "bd_zeroed"))
        c_ready, c_stored, c_loaded = (sem(s) for s in ("c_ready", "c_stored", "c_loaded"))
        parts_ready, out_stored = sem("parts_ready"), [sem("out_stored0"), sem("out_stored1")]

        def wait_apart(engine, *counts):
            counts = [(s, v if isinstance(v, int) else engine.to_reg(v)) for s, v in counts]
            engine.wait_ge(const_ready, 1)
            for s, v in counts:
                wait(engine, s, v)

        def names(prefix, words):
            return {w: sem(f"{prefix}_{w}") for w in words.split()}

        common = "stat var veps rstd xn ctx0 ctx1 tr xct "
        a = names("a", common + "q k v0 qf kf hq hk vc qs bd ks s mx e rd nm t pt0 pt1 pv oT o x")
        c = names("c", common + "v vc y yc s mx e rd nm t pt0 pt1 pv oT o x")
        b = names("b", common + "lg lgc top topi topf d e g comb h hr y yacc x step")
        d = names("d", "stat var veps rstd xn tr xct h hr y x")

        block = ctx.enter_context(nc.Block())
        x_v = x.rearrange("b s d -> s b d")
        flat_mask = mask_keys.rearrange("b s -> (b s)")

        def norm_dve_stats(dve, s, prev_x, m, p):
            if prev_x is not None:
                wait(dve, prev_x, m + 1)
            nc.vector.bn_stats(stats[:, p, :], X[:, m, :]).then_inc(s["stat"], 1)
            wait_apart(dve, (s["stat"], m + 1), (s["rstd"], m - 1))
            nc.vector.bn_aggr(mv[:, p, :], stats[:, p, :]).then_inc(s["var"], 1)

        def norm_pool(pool, s, m, p):
            p = 2 if s is d else p
            wait_apart(pool, (s["var"], m + 1))
            nc.gpsimd.tensor_scalar(veps[:, p, :], mv[:, p, 1:2], EPS, None, ALU.add).then_inc(s["veps"], 1)
            wait(pool, s["veps"], m + 1)
            wait(pool, s["xn"], m if s is d else m - 1)
            nc.gpsimd.tensor_tensor(rstd[:, p, :], veps[:, p, :], expo[:], ALU.pow).then_inc(s["rstd"], 1)

        def norm_dve_apply(dve, s, m, p):
            wait(dve, s["rstd"], m + 1)
            wait(dve, s["tr"], m - 1)
            nc.vector.tensor_scalar(XN[:, p, :], X[:, m, :], mv[:, p, 0:1], rstd[:, p, :],
                                    ALU.subtract, ALU.mult).then_inc(s["xn"], 1)

        def load_ctx(sp, s, m, p):
            wait(sp, s["tr"], m - 1)
            sp.dma_start(CX[:, p, :], ctx_in[m]).then_inc(s[f"ctx{p}"], 16)

        def scale_pool(pool, s, m, p, g):
            wait(pool, s["rd"], NU * m + g + 1)
            unit = PR[:, g, :].rearrange("p (j k) -> p j k", j=G)
            nc.gpsimd.tensor_tensor(unit, unit, rden[:, p, G * g:G * g + G].unsqueeze(2).broadcast_to([P, G, P]),
                                    ALU.mult).then_inc(s["nm"], 1)

        def diagonal(p):
            first = VZ[:, p, :, 0:DH0]
            (row, (step, count), inner) = first.ap
            return bass.AP(first.tensor, first.offset, [row, [step + DH0, count], inner])

        def scaled_units(n, p):
            return [(n - 1, 1 - p, NU - 1)] + [(n, p, g) for g in range(NU - 1)]

        def slots(n, p):
            q = 1 - p
            return [((n, p, k), (n - 1, q, k + 2) if k < 2 else (n, p, k - 2), (n - 1, q, k + 1) if k < 3 else (n, p, 0))
                    for k in range(NU)]

        @block.sync
        def _(sp):
            for src, i in ((wq0, 0), (wk0, 1), (wv0, 2), (wo0, 3)):
                sp.dma_start(nat0[:, i, :], src).then_inc(ld_w0, 16)
            sp.dma_start(mq_i[:], mask_queries).then_inc(ld_setup, 16)
            for i, src in enumerate((bv0, bo0, bout1, ffn_b2)):
                sp.dma_start(brow_f[0:1, i, 0, :], src.unsqueeze(0)).then_inc(ld_setup, 16)
            for j in range(G):
                for r in range(REPS):
                    rows = slice((j * REPS + r) * DH0, (j * REPS + r + 1) * DH0)
                    for i, src in enumerate((bq0, bk0)):
                        sp.dma_start(bqk[rows, i, :], src.rearrange("(g j d) -> j d g", g=NU, j=G)[j]).then_inc(ld_setup, 16)
            for k in range(4):
                sp.dma_start(X[:, 8 * k:8 * k + 8, :], x_v[:, 8 * k:8 * k + 8, :]).then_inc(ld_x, 16)
            sp.dma_start(mk_bc[:], flat_mask.partition_broadcast(P)).then_inc(ld_setup, 16)
            sp.dma_start(mk3[:], flat_mask.partition_broadcast(3)).then_inc(ld_setup, 16)
            sp.wait_ge(parts_ready, 1)
            for r in range(3):
                sp.dma_start(brow[r:r + 1, :, :], brow_b[0:1, :, r, :]).then_inc(rows_moved, 16)

            def step0(n, p):
                if exists(n + 2):
                    load_ctx(sp, a, n + 2, p)
                if exists(n + 1):
                    m = n + 1
                    wait_apart(sp, (a["ks"], m + 1), (a["s"], NU * (m - 1)))
                    for j in range(G):
                        rows = slice(j * REPS * DH0, (j + 1) * REPS * DH0)
                        sp.dma_start(KBD[rows, 1 - p, :, j, :].bitcast(FP32), KS[rows, :, :].bitcast(FP32)).then_inc(a["bd"], 16)

            sp.wait_ge(c_ready, 1)
            sp.dma_start(c_dram, mq_b[:]).then_inc(c_stored, 16)
            sp.wait_ge(c_stored, 16)
            sp.dma_start(c_rows[:].rearrange("r (b s) -> r b s", b=NB), c_dram.rearrange("b r s -> r b s")).then_inc(c_loaded, 16)
            sp.wait_ge(bd_zeroed, 1)
            over_steps(sp, step0, -2, NB, 2)

            def step1(n, p):
                if exists(n + 2):
                    load_ctx(sp, c, n + 2, p)
                if exists(n - 2):
                    wait(sp, d["x"], n - 1)
                    sp.dma_start(out[n - 2], acc[:, p, :]).then_inc(out_stored[p], 16)
            over_steps(sp, step1, -2, NB + 1, 2)
            sp.wait_ge(out_stored[0], 8 * NB)
            sp.wait_ge(out_stored[1], 8 * NB)

        @block.gpsimd
        def _(pool):
            nc.gpsimd.memset(ident[:], 0.0).then_inc(pool_self, 1)
            nc.gpsimd.memset(ones_row[:], 1.0)
            nc.gpsimd.memset(ones3[:], 1.0)
            nc.gpsimd.memset(expo[:], -0.5)
            nc.gpsimd.iota(iota8[:], [[1, NE]], base=0, channel_multiplier=0, allow_small_or_imprecise_dtypes=True)
            for k in range(3):
                nc.gpsimd.memset(patt[0:1, 4, k:k + 1], bf16_parts(FILL0)[k])
            nc.gpsimd.memset(patt[0:1, 4, 3:], 0.0)
            for k, low in ((0, (2, 3)), (1, (1, 3))):
                row = patt[0:1, 2 * k:2 * k + 2, :].rearrange("o k (j r d) -> o k j r d", j=G, r=REPS)
                for r in range(REPS):
                    nc.gpsimd.memset(row[:, 0, :, r, :], -1.0 if r in low else 1.0)
                    nc.gpsimd.memset(row[:, 1, :, r, :], 1.0 if r in low else 0.0)
            pool.wait_ge(pool_self, 1)
            nc.gpsimd.affine_select(out=ident[:], in_=ident[:], compare_op=ALU.not_equal, fill=1.0, base=0,
                                    pattern=[[-1, P]], channel_multiplier=1).then_inc(pool_self, 1)
            pool.wait_ge(pool_self, 2)
            nc.gpsimd.memset(one1[:], 1.0).then_inc(const_ready, 1)
            nc.gpsimd.memset(KBD[:].rearrange("p a g j s -> p (a g j s)").bitcast(FP32), 0.0).then_inc(bd_zeroed, 1)

            def step0(n, p):
                for k, (m, r, g) in enumerate(scaled_units(n, p)):
                    if exists(m):
                        scale_pool(pool, a, m, r, g)
                    if k == 0 and exists(n + 2):
                        norm_pool(pool, a, n + 2, p)
            over_steps(pool, step0, -2, NB, 2)

            def stepb(n, p):
                if has_norm(n):
                    norm_pool(pool, b, n + 2, p)
            norm_pool(pool, b, 0, 0)
            over_items(pool, stepb)

            def step1(n, p):
                for k, (m, r, g) in enumerate(scaled_units(n, p)):
                    if exists(m):
                        scale_pool(pool, c, m, r, g)
                    if k == 0 and exists(n - 2):
                        norm_pool(pool, d, n - 2, p)
                    if k == 1 and exists(n + 2):
                        norm_pool(pool, c, n + 2, p)
            over_steps(pool, step1, -2, NB + 1, 2)

        @block.scalar
        def _(act):
            for t, src in ((gw[:], gate_w), (w1[:], moe_w1.rearrange("e d h -> d e h")),
                           (w2[:], moe_w2.rearrange("e (c p) d -> p e c d", p=P)), (f1[:], ffn_w1),
                           (f2[:], ffn_w2.rearrange("(c p) d -> p c d", p=P)), (fb1[:], ffn_b1.rearrange("(c p) -> p c", p=P))):
                act.dma_start(t, src).then_inc(ld_ffn, 16)
            for t, src in ((nat1[:, 0, :], wq1), (nat1[:, 1, :], wkv1[:, 0:INNER]), (wv1[:], wkv1[:, INNER:]),
                           (wout[:], wout1.rearrange("(c p) d -> p c d", p=P))):
                act.dma_start(t, src).then_inc(ld_w1, 16)

            def read_xct(s, m, p, both, free_sem, free_count):
                M_BANK = M2_BANK if s is a else bank[7]
                act.wait_ge(s["tr"], m + 1)
                wait(act, free_sem, free_count)
                k = 2 if both else 1
                nc.scalar.activation(XCT[:, p, 0:k, :], M_BANK[:, 0:k * P].rearrange("p (k s) -> p k s", k=k),
                                     ACT.Copy).then_inc(s["xct"], 1)

            def exponentials(s, m, p, g):
                wait_apart(act, (s["mx"], NU * m + g + 1), (s["t"], NU * (m - 1) + g + 1))
                for j in range(G):
                    h = G * g + j
                    last = nc.scalar.activation(PR[:, g, j * P:(j + 1) * P], S_BANK[g % 2][:, j * P:(j + 1) * P], ACT.Exp,
                                                bias=nmx[:, p, h:h + 1], accum_out=den[:, p, h:h + 1])
                last.then_inc(s["e"], 1)

            def read_PT(s, m, g):
                act.wait_ge(s["t"], NU * m + g + 1)
                wait(act, s["pv"], NU * m + g - 1)
                nc.scalar.activation(PT[:, g % 2, :], T_BANK[g % 2][:], ACT.Copy).then_inc(s["pt1"], 1)

            def step0(n, p):
                q, m = 1 - p, n + 1
                if exists(m):
                    read_xct(a, m, q, True, a["v0"], m - 1)
                if exists(n):
                    exponentials(a, n, p, 0)
                    exponentials(a, n, p, 1)
                if exists(n - 1):
                    read_PT(a, n - 1, 3)
                if exists(m):
                    act.wait_ge(a["q"], m + 1)
                    wait(act, a["qs"], m)
                    for g in range(NU):
                        last = nc.scalar.activation(QF[:, 0, g, :], bank[4][:, g * P:(g + 1) * P], ACT.Identity,
                                                    bias=bqk[:, 0, g:g + 1], scale=float(DH0) ** -0.5)
                    last.then_inc(a["qf"], 1)
                    act.wait_ge(a["qf"], m + 1)
                    nc.scalar.activation(HF[:, 0, :, :].bitcast(FP32R), QF[:, 0, :, :], ACT.Copy,
                                         scale=pcol[:, 0:1]).then_inc(a["hq"], 1)
                if exists(n):
                    exponentials(a, n, p, 2)
                if exists(n - 1):
                    act.wait_ge(a["pv"], NU * n)
                    wait(act, a["o"], n - 2)
                    nc.scalar.activation(OT[:, q, 0, :], bank[6][:, 0:P], ACT.Copy).then_inc(a["oT"], 1)
                if exists(n):
                    exponentials(a, n, p, 3)
                    read_PT(a, n, 1)
                if exists(m):
                    act.wait_ge(a["v0"], m + 1)
                    wait(act, a["pv"], NU * (m - 1))
                    nc.scalar.activation(diagonal(q), M_BANK[:, 0:P].rearrange("p (h d) -> p h d", h=NH),
                                         ACT.Copy).then_inc(a["vc"], 1)
            over_steps(act, step0, -2, NB, 2)

            def stepb(n, p):
                if has_front(n):
                    read_xct(b, n + 1, 1 - p, False, b["h"], NE * n)
                if has_back(n):
                    act.wait_ge(b["d"], n + 1)
                    nc.scalar.activation(gcol[:, p, 1:2], gcol[:, p, 0:1], ACT.Exp).then_inc(b["e"], 1)
                    for e in range(NE):
                        u = NE * n + e
                        act.wait_ge(b["h"], u + 1)
                        wait(act, b["y"], u - 1)
                        nc.scalar.activation(H[:, e % 2, :, :].rearrange("p c s -> p (c s)"), bank[e % 2][:],
                                             ACT.Relu).then_inc(b["hr"], 1)
            over_items(act, stepb)

            def step1(n, p):
                q, m = 1 - p, n + 1

                def read_v(half):
                    act.wait_ge(c["v"], 2 * m + half + 1)
                    wait(act, c["pv"], NU * (m - 1))
                    nc.scalar.activation(V1[:, q, 8 * half:8 * half + 8, :], bank[4][:].rearrange("p (h d) -> p h d", h=8),
                                         ACT.Copy).then_inc(c["vc"], 1)

                def read_heads(half):
                    act.wait_ge(c["pv"], NU * (n - 1) + 2 * half + 2)
                    wait(act, c["o"], n - 2)
                    nc.scalar.activation(OT[:, q, 4 * half:4 * half + 4, :].rearrange("p c s -> p (c s)"), bank[5 + half][:],
                                         ACT.Copy).then_inc(c["oT"], 1)

                if exists(m):
                    read_xct(c, m, q, True, c["s"], NU * (m - 1))
                if exists(n):
                    exponentials(c, n, p, 0)
                if exists(n - 1):
                    read_heads(0)
                if exists(n):
                    exponentials(c, n, p, 1)
                if exists(n - 1):
                    read_PT(c, n - 1, 3)
                if exists(n):
                    exponentials(c, n, p, 2)
                if exists(n - 1):
                    read_heads(1)
                if exists(m):
                    read_v(0)
                if exists(n):
                    exponentials(c, n, p, 3)
                    read_PT(c, n, 1)
                if exists(m):
                    read_v(1)
            over_steps(act, step1, -2, NB + 1, 2)

        @block.vector
        def _(dve):
            chain = [0]

            def link(ins):
                chain[0] += 1
                ins.then_inc(dve_self, 1)
                dve.wait_ge(dve_self, chain[0])

            dve.wait_ge(ld_setup, 16 * (5 + 2 * G * REPS + 2))
            link(nc.vector.tensor_copy(brow_b[:, :, 0, :], brow_f[:, 0:4, 0, :]))
            link(nc.vector.tensor_tensor(brow_f[:, 0:4, 1, :], brow_f[:, 0:4, 0, :], brow_b[:, :, 0, :], ALU.subtract))
            link(nc.vector.tensor_copy(brow_b[:, :, 1, :], brow_f[:, 0:4, 1, :]))
            nc.vector.tensor_tensor(brow_b[:, :, 2, :], brow_f[:, 0:4, 1, :], brow_b[:, :, 1, :],
                                    ALU.subtract).then_inc(parts_ready, 1)
            link(nc.vector.tensor_scalar(mq_f[:, 0, :], mq_i[:], -1.0, 1.0, ALU.mult, ALU.add))
            link(nc.vector.tensor_scalar(mq_f[:, 1, :], mq_f[:, 0, :], -FILL1, None, ALU.mult))
            link(nc.vector.tensor_copy(mq_b[:, 0, :], mq_f[:, 1, :]))
            link(nc.vector.tensor_tensor(mq_f[:, 2, :], mq_f[:, 1, :], mq_b[:, 0, :], ALU.subtract))
            link(nc.vector.tensor_copy(mq_b[:, 1, :], mq_f[:, 2, :]))
            nc.vector.tensor_tensor(mq_b[:, 2, :], mq_f[:, 2, :], mq_b[:, 1, :], ALU.subtract).then_inc(c_ready, 1)
            dve.wait_ge(set_pe, 1)
            link(nc.vector.tensor_copy(pcol[:], bank[0][:, 0:5]))
            nc.vector.tensor_scalar(mk_rows[:], mk3[:], -1.0, pcol[0:3, 4:5], ALU.add, ALU.mult)
            dve.wait_ge(set_pe, 2)
            for i in range(2):
                src = bank[1][:, i * P:(i + 1) * P].rearrange("p (g j d) -> p g j d", g=NU, j=G)
                dst = wqk_rep[:, i, :, :].rearrange("p g (j r d) -> p g j r d", j=G, r=REPS)
                for r in range(REPS):
                    for g in range(NU):
                        nc.vector.tensor_copy(dst[:, g, :, r, :], src[:, g, :, :])
            nc.vector.tensor_copy(wv0T[:], bank[1][:, 2 * P:3 * P])
            nc.vector.tensor_copy(wo0T[:], bank[1][:, 3 * P:4 * P])
            link(nc.vector.tensor_scalar(bqk[:, 0, :], bqk[:, 0, :], float(DH0) ** -0.5, None, ALU.mult))
            nc.vector.memset(den[:, 0, :], 0.0).then_inc(set_copy, 1)
            for t in range(2 * PAIRS // 4):
                dve.wait_ge(set_pe, 3 + t)
                i, k = t // 2, 4 * (t % 2)
                nc.vector.tensor_copy(qkT[:, i, k:k + 4, :].rearrange("p c s -> p (c s)"), bank[2 + t % 2][:]).then_inc(set_copy, 1)
            for g in range(NU):
                dve.wait_ge(set_pe, 7 + g)
                even_odd = A[:, 8 * (g // 2):8 * (g // 2) + 8, :].rearrange("p (j o) s -> p o j s", o=2)
                nc.vector.tensor_scalar(even_odd[:, g % 2], bank[2 + g % 2][:].rearrange("p (j s) -> p j s", j=G),
                                        float(DH1) ** -0.5, None, ALU.mult).then_inc(set_copy, 1)
            SETUP_COPIES = 1 + 4 + NU
            dve.wait_ge(set_copy, SETUP_COPIES)
            link(nc.vector.memset(VZ[:], 0.0))
            dve.wait_ge(ld_x, 64)

            def row_max(s, m, p, g):
                dve.wait_ge(s["s"], NU * m + g + 1)
                nc.vector.tensor_reduce(nmx[:, p, G * g:G * g + G], S_BANK[g % 2][:].rearrange("p (j k) -> p j k", j=G),
                                        AXX, ALU.max, negate=True).then_inc(s["mx"], 1)

            def sums_reciprocal(s, m, p, g):
                dve.wait_ge(s["e"], NU * m + g + 1)
                nc.vector.reciprocal(rden[:, p, G * g:G * g + G], den[:, p, G * g:G * g + G]).then_inc(s["rd"], 1)

            def read_PT(s, m, g):
                dve.wait_ge(s["t"], NU * m + g + 1)
                wait(dve, s["pv"], NU * m + g - 1)
                nc.vector.tensor_copy(PT[:, g % 2, :], T_BANK[g % 2][:]).then_inc(s["pt0"], 1)

            def step0(n, p):
                q, m = 1 - p, n + 1
                if exists(n):
                    row_max(a, n, p, 0)
                if exists(n - 1):
                    sums_reciprocal(a, n - 1, q, 3)
                if exists(n + 2):
                    norm_dve_stats(dve, a, None, n + 2, p)
                if exists(n - 1):
                    read_PT(a, n - 1, 2)
                if exists(n):
                    row_max(a, n, p, 1)
                    sums_reciprocal(a, n, p, 0)
                if exists(m):
                    dve.wait_ge(a["k"], m + 1)
                    for g in range(NU):
                        last = nc.vector.scalar_tensor_tensor(QF[:, 1, g, :], bank[4][:, g * P:(g + 1) * P],
                                                              bqk[:, 1, g:g + 1], mk_bc[:, bass.ds(m * P, P)],
                                                              ALU.add, ALU.mult)
                    last.then_inc(a["kf"], 1)
                    dve.wait_ge(a["kf"], m + 1)
                    nc.vector.tensor_scalar(HF[:, 1, :, :].bitcast(FP32R), QF[:, 1, :, :], pcol[:, 2:3], None,
                                            ALU.mult).then_inc(a["hk"], 1)
                    dve.wait_ge(a["hk"], m + 1)
                    wait(dve, a["bd"], 16 * G * m)
                    nc.vector.scalar_tensor_tensor(KS[:], QF[:, 1, :, :], pcol[:, 3:4], HF[:, 1, :, :],
                                                   ALU.mult, ALU.add).then_inc(a["ks"], 1)
                if exists(n):
                    row_max(a, n, p, 2)
                    sums_reciprocal(a, n, p, 1)
                    read_PT(a, n, 0)
                if exists(m):
                    dve.wait_ge(a["hq"], m + 1)
                    wait(dve, a["s"], NU * (m - 1))
                    nc.vector.scalar_tensor_tensor(QS[:, q, :, :], QF[:, 0, :, :], pcol[:, 1:2], HF[:, 0, :, :],
                                                   ALU.mult, ALU.add).then_inc(a["qs"], 1)
                if exists(n):
                    row_max(a, n, p, 3)
                    sums_reciprocal(a, n, p, 2)
                if exists(n + 2):
                    norm_dve_apply(dve, a, n + 2, p)
                if exists(n - 1):
                    dve.wait_ge(a["o"], n)
                    xrow = X[:, bass.ds(n - 1, 1), :].rearrange("p o d -> p (o d)")
                    nc.vector.tensor_tensor(xrow, M2_BANK[:, 0:P], xrow, ALU.add).then_inc(a["x"], 1)
            over_steps(dve, step0, -2, NB, 2)

            norm_dve_stats(dve, b, a["x"], 0, 0)
            norm_dve_apply(dve, b, 0, 0)

            def stepb(n, p):
                if has_norm(n):
                    norm_dve_stats(dve, b, a["x"], n + 2, p)
                    norm_dve_apply(dve, b, n + 2, p)
                if has_back(n):
                    dve.wait_ge(b["lg"], n + 1)
                    nc.vector.tensor_copy(lg[:, p, :], bank[6][:, 0:NE]).then_inc(b["lgc"], 1)
                    wait_apart(dve, (b["lgc"], n + 1))
                    nc.vector.max(top[:, p, :], lg[:, p, :]).then_inc(b["top"], 1)
                    dve.wait_ge(b["top"], n + 1)
                    nc.vector.tensor_tensor(gcol[:, p, 0:1], top[:, p, 1:2], top[:, p, 0:1], ALU.subtract).then_inc(b["d"], 1)
                    nc.vector.max_index(topi[:, p, :], top[:, p, :], lg[:, p, :]).then_inc(b["topi"], 1)
                    dve.wait_ge(b["topi"], n + 1)
                    nc.vector.tensor_copy(topf[:, p, :], topi[:, p, 0:2]).then_inc(b["topf"], 1)
                    dve.wait_ge(b["e"], n + 1)
                    nc.vector.tensor_scalar(gcol[:, p, 2:3], gcol[:, p, 1:2], 1.0, None, ALU.add).then_inc(b["g"], 1)
                    dve.wait_ge(b["g"], 3 * n + 1)
                    nc.vector.reciprocal(gcol[:, p, 3:4], gcol[:, p, 2:3]).then_inc(b["g"], 1)
                    dve.wait_ge(b["g"], 3 * n + 2)
                    nc.vector.tensor_tensor(gcol[:, p, 4:5], gcol[:, p, 3:4], gcol[:, p, 1:2], ALU.mult).then_inc(b["g"], 1)
                    dve.wait_ge(b["topf"], n + 1)
                    dve.wait_ge(b["g"], 3 * n + 3)
                    for k in range(2):
                        last = nc.vector.tensor_scalar(comb[:, p, k, :], iota8[:], topf[:, p, k:k + 1], gcol[:, p, 3 + k:4 + k],
                                                       ALU.is_equal, ALU.mult)
                    last.then_inc(b["comb"], 1)
                    dve.wait_ge(b["comb"], 2 * n + 1)
                    nc.vector.tensor_tensor(comb[:, p, 0, :], comb[:, p, 0, :], comb[:, p, 1, :], ALU.add).then_inc(b["comb"], 1)
                    dve.wait_ge(b["comb"], 2 * n + 2)
                    xrow = X[:, bass.ds(n, 1), :].rearrange("p o d -> p (o d)")
                    for e in range(NE):
                        u = NE * n + e
                        dve.wait_ge(b["y"], u + 1)
                        if e:
                            dve.wait_ge(b["yacc"], u)
                        nc.vector.scalar_tensor_tensor(xrow if e == NE - 1 else acc[:, e % 2, :], bank[4 + e % 2][:, 0:P],
                                                       comb[:, p, 0, e:e + 1], acc[:, (e + 1) % 2, :] if e else xrow,
                                                       ALU.mult, ALU.add).then_inc(b["yacc"], 1)
            over_items(dve, stepb)

            def step1(n, p):
                q, m = 1 - p, n + 1

                def read_y(g):
                    dve.wait_ge(c["y"], NU * m + g + 1)
                    wait(dve, c["s"], NU * (m - 1))
                    nc.vector.tensor_copy(YT[:, q, G * g:G * g + G, :].rearrange("p h s -> p (h s)"),
                                          bank[4][:]).then_inc(c["yc"], 1)

                if exists(n - 2):
                    wait_apart(dve, (c["x"], n - 1))
                    nc.vector.bn_stats(stats[:, 2, :], X[:, bass.ds(n - 2, 1), :].rearrange("p o d -> p (o d)")).then_inc(d["stat"], 1)
                    wait_apart(dve, (d["stat"], n - 1), (d["rstd"], n - 2))
                    nc.vector.bn_aggr(mv[:, 2, :], stats[:, 2, :]).then_inc(d["var"], 1)
                if exists(n):
                    row_max(c, n, p, 0)
                if exists(n - 1):
                    sums_reciprocal(c, n - 1, q, 3)
                if exists(n + 2):
                    norm_dve_stats(dve, c, None, n + 2, p)
                if exists(n - 1):
                    read_PT(c, n - 1, 2)
                if exists(n - 2):
                    wait(dve, d["rstd"], n - 1)
                    wait(dve, d["tr"], n - 2)
                    nc.vector.tensor_scalar(XND[:], X[:, bass.ds(n - 2, 1), :].rearrange("p o d -> p (o d)"), mv[:, 2, 0:1],
                                            rstd[:, 2, :], ALU.subtract, ALU.mult).then_inc(d["xn"], 1)
                if exists(m):
                    read_y(0)
                if exists(n):
                    row_max(c, n, p, 1)
                if exists(m):
                    read_y(1)
                if exists(n):
                    sums_reciprocal(c, n, p, 0)
                if exists(n - 2):
                    dve.wait_ge(d["tr"], n - 1)
                    wait(dve, d["h"], n - 2)
                    nc.vector.tensor_copy(XDT[:], bank[7][:, 0:P]).then_inc(d["xct"], 1)
                if exists(m):
                    read_y(2)
                if exists(n):
                    row_max(c, n, p, 2)
                if exists(n - 2):
                    dve.wait_ge(d["h"], n - 1)
                    wait(dve, d["y"], n - 2)
                    for k in range(HC):
                        last = nc.vector.tensor_scalar(H[:, 0, k, :], bank[4][:, k * P:(k + 1) * P], fb1[:, k:k + 1], 0.0,
                                                       ALU.add, ALU.max)
                    last.then_inc(d["hr"], 1)
                if exists(n):
                    sums_reciprocal(c, n, p, 1)
                    read_PT(c, n, 0)
                if exists(m):
                    read_y(3)
                if exists(n):
                    row_max(c, n, p, 3)
                    sums_reciprocal(c, n, p, 2)
                if exists(n + 2):
                    norm_dve_apply(dve, c, n + 2, p)
                if exists(n - 2):
                    dve.wait_ge(d["y"], n - 1)
                    wait(dve, out_stored[p], loads(n - 4, p))
                    nc.vector.tensor_tensor(acc[:, p, :], bank[7][:, 0:P],
                                            X[:, bass.ds(n - 2, 1), :].rearrange("p o d -> p (o d)"),
                                            ALU.add).then_inc(d["x"], 1)
                if exists(n - 1):
                    dve.wait_ge(c["o"], n)
                    xrow = X[:, bass.ds(n - 1, 1), :].rearrange("p o d -> p (o d)")
                    nc.vector.tensor_tensor(xrow, bank[7][:, 0:P], xrow, ALU.add).then_inc(c["x"], 1)
            over_steps(dve, step1, -2, NB + 1, 2)

        @block.tensor
        def _(pe):
            mm = nc.tensor.matmul
            pe.wait_ge(const_ready, 1)
            for k in range(5):
                last = mm(bank[0][:, k:k + 1], patt[0:1, k, :], one1[:], start=True, stop=True)
            last.then_inc(set_pe, 1)
            pe.wait_ge(ld_w0, 64)
            for i in range(4):
                last = nc.tensor.transpose(bank[1][:, i * P:(i + 1) * P], nat0[:, i, :], ident[:])
            last.then_inc(set_pe, 1)
            pe.wait_ge(ld_w1, 64)
            for t in range(2 * PAIRS // 4):
                i, k = t // 2, 4 * (t % 2)
                if t >= 2:
                    pe.wait_ge(set_copy, 1 + t - 1)
                for j in range(4):
                    last = nc.tensor.transpose(bank[2 + t % 2][:, j * P:(j + 1) * P], nat1[:, i, (k + j) * P:(k + j + 1) * P], ident[:])
                last.then_inc(set_pe, 1)
            for g in range(NU):
                pe.wait_ge(set_copy, 1 + 4 + max(0, g - 1))
                for j in range(G):
                    h = 8 * (g // 2) + 2 * j + g % 2
                    rows = slice(DH1 * (h % 2), DH1 * (h % 2 + 1))
                    last = mm(bank[2 + g % 2][:, j * P:(j + 1) * P], qkT[rows, 0, h // 2, :], qkT[rows, 1, h // 2, :],
                              start=True, stop=True)
                last.then_inc(set_pe, 1)
            pe.wait_ge(set_copy, 1 + 4 + NU)
            pe.wait_ge(rows_moved, 48)

            def transpose_in(s, m, p, both, m_free, m_count):
                M_BANK = M2_BANK if s is a else bank[7]
                pe.wait_ge(s["xn"], m + 1)
                if both:
                    pe.wait_ge(s[f"ctx{p}"], loads(m, p))
                wait(pe, m_free, m_count)
                last = nc.tensor.transpose(M_BANK[:, 0:P], XN[:, p, :], ident[:])
                if both:
                    last = nc.tensor.transpose(M_BANK[:, P:2 * P], CX[:, p, :], ident[:])
                last.then_inc(s["tr"], 1)

            def transpose_unit(s, m, g):
                wait(pe, s["nm"], NU * m + g + 1)
                wait(pe, s[f"pt{g % 2}"], 2 * m + g // 2)
                for j in range(G):
                    last = nc.tensor.transpose(T_BANK[g % 2][:, j * P:(j + 1) * P], PR[:, g, j * P:(j + 1) * P], ident[:])
                last.then_inc(s["t"], 1)

            def step0(n, p):
                q, m = 1 - p, n + 1

                def scores(m, p, g):
                    waits = [(a["e"], NU * m + g - 1)]
                    if g == 0:
                        waits += [(a["qs"], m + 1), (a["bd"], 16 * G * (m + 1))]
                    wait_apart(pe, *waits)
                    mm(S_BANK[g % 2][:].rearrange("p (j k) -> p j k", j=G), ones3[:],
                       mk_rows[:, bass.ds(m * P, P)].unsqueeze(1).broadcast_to([3, G, P]), start=True, stop=False,
                       skip_group_check=True)
                    mm(S_BANK[g % 2][:], QS[:, p, g, :], KBD[:, p, g, :, :].rearrange("p j s -> p (j s)"),
                       start=False, stop=True, skip_group_check=True).then_inc(a["s"], 1)

                def values(m, p, g):
                    wait(pe, a[f"pt{g % 2}"], 2 * m + g // 2 + 1)
                    if g == 0:
                        pe.wait_ge(a["vc"], m + 1)
                        wait(pe, a["oT"], m)
                    for j in range(G):
                        h = G * g + j
                        last = mm(bank[6][:, 0:P], VZ[:, p, h, :], PT[:, g % 2, j * P:(j + 1) * P],
                                  start=(h == 0), stop=(h == NH - 1))
                    last.then_inc(a["pv"], 1)

                def project(i, name, free_sem, free_count):
                    pe.wait_ge(a["xct"], m + 1)
                    wait(pe, free_sem, free_count)
                    for g in range(NU):
                        last = mm(bank[4][:, g * P:(g + 1) * P], wqk_rep[:, i, g, :], XCT[:, q, i, :], start=True, stop=True)
                    last.then_inc(a[name], 1)

                for k, (scored, turned, used) in enumerate(slots(n, p)):
                    if exists(scored[0]):
                        scores(*scored)
                    if k == 0 and exists(m):
                        transpose_in(a, m, q, True, *((a["xct"], m) if isinstance(n, int) and n < 2 else (a["x"], n - 1)))
                    if k == 1 and exists(m):
                        project(1, "k", a["qf"], m)
                    if exists(turned[0]):
                        transpose_unit(a, turned[0], turned[2])
                    if k == 3 and exists(m):
                        wait(pe, a["vc"], m)
                        mm(M_BANK[:, 0:P], XCT[:, q, 1, :], wv0T[:], start=True, stop=False)
                        mm(M_BANK[:, 0:P], ones3[:], brow[:, 0, :], start=False, stop=True).then_inc(a["v0"], 1)
                    if exists(used[0]):
                        values(*used)
                    if k == 1 and exists(m):
                        project(0, "q", a["kf"], m + 1)
                    if k == 3 and exists(n - 1):
                        wait(pe, a["oT"], n)
                        if exists(m):
                            pe.wait_ge(a["xct"], m + 1)
                        else:
                            wait(pe, a["x"], n - 1)
                        mm(M2_BANK[:, 0:P], OT[:, q, 0, :], wo0T[:], start=True, stop=False)
                        mm(M2_BANK[:, 0:P], ones3[:], brow[:, 1, :], start=False, stop=True).then_inc(a["o"], 1)
            over_steps(pe, step0, -2, NB, 2)

            pe.wait_ge(ld_ffn, 96)

            def stepb(n, p):
                if has_front(n):
                    transpose_in(b, n + 1, 1 - p, False, b["xct"] if not is_start(n) else a["x"], n + 1 if not is_start(n) else NB)
                if has_back(n):
                    pe.wait_ge(b["xct"], n + 1)
                    wait(pe, b["lgc"], n)
                    mm(bank[6][:, 0:NE], XCT[:, p, 0, :], gw[:], start=True, stop=True).then_inc(b["lg"], 1)

                    def hidden(e):
                        wait(pe, b["hr"], NE * n + e - 1)
                        for k in range(HC):
                            last = mm(bank[e % 2][:, k * P:(k + 1) * P], w1[:, e, k * P:(k + 1) * P], XCT[:, p, 0, :],
                                      start=True, stop=True)
                        last.then_inc(b["h"], 1)

                    hidden(0)
                    for e in range(NE):
                        if e + 1 < NE:
                            hidden(e + 1)
                        pe.wait_ge(b["hr"], NE * n + e + 1)
                        wait(pe, b["yacc"], NE * n + e - 1)
                        for k in range(HC):
                            last = mm(bank[4 + e % 2][:, 0:P], H[:, e % 2, k, :], w2[:, e, k, :], start=(k == 0), stop=(k == HC - 1))
                        last.then_inc(b["y"], 1)
            over_items(pe, stepb)

            pe.wait_ge(c_loaded, 16)
            def step1(n, p):
                q, m = 1 - p, n + 1

                def project_v(half):
                    if half:
                        pe.wait_ge(c["vc"], 2 * m + 1)
                    else:
                        pe.wait_ge(c["yc"], NU * (m + 1))
                    mm(bank[4][:], XCT[:, q, 1, :], wv1[:, 512 * half:512 * half + 512], start=True, stop=True).then_inc(c["v"], 1)

                def project_y(g):
                    if g == 0:
                        pe.wait_ge(c["xct"], m + 1)
                        wait(pe, c["vc"], 2 * m)
                    else:
                        pe.wait_ge(c["yc"], NU * m + g)
                        if g == 3 and exists(n - 2):
                            pe.wait_ge(d["hr"], n - 1)
                    for j in range(G):
                        last = mm(bank[4][:, j * P:(j + 1) * P], A[:, G * g + j, :], XCT[:, q, 0, :], start=True, stop=True)
                    last.then_inc(c["y"], 1)

                def scores(m, p, g):
                    wait(pe, c["yc"], NU * m + g + 1)
                    wait(pe, c["e"], NU * m + g - 1)
                    for j in range(G):
                        mm(S_BANK[g % 2][:, j * P:(j + 1) * P], YT[:, p, G * g + j, :], XCT[:, p, 1, :], start=(j == 0), stop=False,
                           skip_group_check=True)
                    mm(S_BANK[g % 2][:], c_rows[:, bass.ds(m * P, P)], ones_row[:], start=False, stop=True,
                       skip_group_check=True).then_inc(c["s"], 1)

                def values(m, p, g):
                    wait(pe, c[f"pt{g % 2}"], 2 * m + g // 2 + 1)
                    if g == 0:
                        pe.wait_ge(c["vc"], 2 * m + 2)
                    if g % 2 == 0:
                        wait(pe, c["oT"], 2 * (m - 1) + g // 2 + 1)
                    for j in range(G):
                        h = G * g + j
                        rows = slice(DH1 * (j % 2), DH1 * (j % 2 + 1))
                        cols = 2 * P * (g % 2) + P * (j // 2)
                        last = mm(bank[5 + g // 2][rows, cols:cols + P], V1[:, p, h, :], PT[:, g % 2, j * P:(j + 1) * P],
                                  start=True, stop=True)
                    last.then_inc(c["pv"], 1)

                for k, (scored, turned, used) in enumerate(slots(n, p)):
                    if exists(scored[0]):
                        scores(*scored)
                    if k == 0 and exists(m):
                        if is_first(n):
                            pe.wait_ge(b["yacc"], NE * NB)
                        transpose_in(c, m, q, True, *((c["xct"], m) if isinstance(n, int) and n < 1 else (c["x"], n - 1)))
                    if k == 1 and exists(m):
                        project_y(1)
                    if k == 3 and exists(m):
                        project_v(0)
                    if k == 2 and exists(n - 2):
                        wait(pe, d["xct"], n - 1)
                        if exists(m):
                            pe.wait_ge(c["yc"], NU * m + 3)
                        else:
                            pe.wait_ge(c["vc"], 2 * NB)
                            pe.wait_ge(d["hr"], n - 2)
                        for kk in range(HC):
                            last = mm(bank[4][:, kk * P:(kk + 1) * P], f1[:, kk * P:(kk + 1) * P], XDT[:], start=True, stop=True)
                        last.then_inc(d["h"], 1)
                    if exists(turned[0]):
                        transpose_unit(c, turned[0], turned[2])
                    if k == 0 and exists(m):
                        project_y(0)
                    if k == 1 and exists(n - 2):
                        wait(pe, d["xn"], n - 1)
                        if exists(m):
                            pe.wait_ge(c["xct"], m + 1)
                        else:
                            wait(pe, c["x"], min(n - 1, NB))
                        nc.tensor.transpose(bank[7][:, 0:P], XND[:], ident[:]).then_inc(d["tr"], 1)
                    if k == 2 and exists(m):
                        project_y(3)
                    if k == 3 and exists(n - 2):
                        wait(pe, d["hr"], n - 1)
                        wait(pe, d["xct"], n - 1)
                        for kk in range(HC):
                            mm(bank[7][:, 0:P], H[:, 0, kk, :], f2[:, kk, :], start=(kk == 0), stop=False)
                        mm(bank[7][:, 0:P], ones3[:], brow[:, 3, :], start=False, stop=True).then_inc(d["y"], 1)
                    if exists(used[0]):
                        values(*used)
                    if k == 1 and exists(m):
                        project_y(2)
                    if k == 3 and exists(n - 1):
                        wait(pe, c["oT"], 2 * n)
                        if exists(n - 2):
                            wait(pe, d["x"], n - 1)
                        elif exists(m):
                            pe.wait_ge(c["xct"], m + 1)
                        for kk in range(PAIRS):
                            mm(bank[7][:, 0:P], OT[:, q, kk, :], wout[:, kk, :], start=(kk == 0), stop=False)
                        mm(bank[7][:, 0:P], ones3[:], brow[:, 2, :], start=False, stop=True).then_inc(c["o"], 1)
                    if k == 3 and exists(m):
                        project_v(1)
            over_steps(pe, step1, -2, NB + 1, 2)


_INS = ["x", "ctx_1024", "mask_BxS2_bf1", "mask_BxS_ik0", "L0_xattn_Wq", "L0_xattn_bq", "L0_xattn_Wk", "L0_xattn_bk",
        "L0_xattn_Wv", "L0_xattn_bv", "L0_xattn_Wo", "L0_xattn_bo", "L0_ffn_w_gate", "L0_ffn_w1", "L0_ffn_w2",
        "L1_xattn_Wq", "L1_xattn_Wkv", "L1_xattn_Wout", "L1_xattn_bout", "L1_ffn_w1", "L1_ffn_b1", "L1_ffn_w2", "L1_ffn_b2"]


def kernel(**inputs):
    import numpy as _np
    import concourse.bacc as _bacc
    from concourse.bass_utils import run_bass_kernel_spmd as _run

    nc = _bacc.Bacc("TRN2", target_bir_lowering=False, num_devices=1)
    arrays, args = {}, []
    for name in _INS:
        a = _np.ascontiguousarray(inputs[name])
        arrays[f"in_{name}_dram"] = a
        args.append(nc.dram_tensor(f"in_{name}_dram", a.shape, mybir.dt.from_np(a.dtype), kind="ExternalInput").ap())
    args.append(nc.dram_tensor("out_0_dram", (NB, P, P), FP32, kind="ExternalOutput").ap())
    args.append(nc.dram_tensor("query_mask_parts", (NB, 3, P), BF16, kind="Internal").ap())
    build(nc, *args)
    r = _run(nc, [arrays], core_ids=[0])
    return r.results[0]["out_0_dram"]
```

```python
import concourse.bass as bass
from concourse import mybir
from contextlib import ExitStack

FP32 = mybir.dt.float32
FP32R = mybir.dt.float32r
BF16 = mybir.dt.bfloat16
U8 = mybir.dt.uint8
U32 = mybir.dt.uint32
I32 = mybir.dt.int32
ALU = mybir.AluOpType
ACT = mybir.ActivationFunctionType
AXX = mybir.AxisListType.X

NB = 32
P = 128
NH = 16
G = 4
NU = NH // G
DH0 = P // NH
DH1 = 64
INNER = NH * DH1
PAIRS = INNER // P
NE = 8
HC = 4
REPS = 4
TILE = 2 * P
REGION = NB * P + TILE
MAX_TILES = 2 * NB * P // TILE + NE
EPS = 1e-5
FILL0 = 1e8
FILL1 = 1e6


def bf16_parts(value):
    import numpy as np
    parts, rest = [], np.float32(value)
    for _ in range(3):
        bits = np.array([rest], np.float32).view(np.uint32)
        part = ((bits + 0x7FFF + ((bits >> 16) & 1)) & 0xFFFF0000).astype(np.uint32).view(np.float32)[0]
        parts.append(float(part))
        rest = np.float32(rest - part)
    return parts


def over_steps(engine, step, first, last, ahead, behind=2):
    loop_start = (behind + 1) // 2
    loop_end = (NB - 1 - ahead) // 2
    for n in range(first, 2 * loop_start):
        step(n, n % 2)
    with engine.Fori(loop_start, loop_end) as i:
        step(i * 2, 0)
        step(i * 2 + 1, 1)
    for n in range(2 * loop_end, last + 1):
        step(n, n % 2)


def exists(m):
    return not isinstance(m, int) or 0 <= m < NB


def loads(m, p):
    return 8 * (m - p) + 16


def is_first(n):
    return isinstance(n, int) and n == -1


def wait(engine, semaphore, value):
    if isinstance(value, int) and value <= 0:
        return
    engine.wait_ge(semaphore, value)


def build(nc, x, ctx_in, mask_keys, mask_queries, wq0, bq0, wk0, bk0, wv0, bv0, wo0, bo0,
          gate_w, moe_w1, moe_w2, wq1, wkv1, wout1, bout1, ffn_w1, ffn_b1, ffn_w2, ffn_b2, out, c_dram, xs, ys):
    ctx = ExitStack()
    with ctx:
        def sb(name, shape, dt=FP32):
            return ctx.enter_context(nc.sbuf_tensor(name, shape, dt))

        def sem(name):
            return ctx.enter_context(nc.semaphore(name))

        ctx.enter_context(nc.allow_non_contiguous_dma(reason="small bias and weight layouts"))
        bank = [ctx.enter_context(nc.psum_tensor(f"bank{i}", [P, 512], FP32)) for i in range(8)]
        S_BANK, T_BANK = bank[0:2], bank[2:4]
        M_BANK, M2_BANK = bank[7], bank[5]

        ident = sb("ident", [P, P])
        ones3 = sb("ones3", [3, P], BF16)
        one1 = sb("one1", [1, 1])
        ones_row = sb("ones_row", [3, 512], BF16)
        expo = sb("expo", [P, 1])
        iota_e = sb("iota_e", [P, NE])
        iota_t = sb("iota_t", [P, NB - 1])
        region = sb("region", [P, NE])
        upper = sb("upper", [P, P], BF16)
        onesb = sb("onesb", [P, P], BF16)
        zero = sb("zero", [P, P])
        X = sb("X", [P, NB, P])
        nat0 = sb("nat0", [P, 4, P])
        wqk_rep = sb("wqk_rep", [P, 2, NU, P])
        wv0T = sb("wv0T", [P, P])
        wo0T = sb("wo0T", [P, P])
        bqk = sb("bqk", [P, 2, NU])
        patt = sb("patt", [1, 5, P])
        pcol = sb("pcol", [P, 5])
        brow_f = sb("brow_f", [1, 5, 3, P])
        brow_b = sb("brow_b", [1, 4, 3, P], BF16)
        brow = sb("brow", [3, 4, P], BF16)
        mk_bc = sb("mk_bc", [P, NB * P], U8)
        mk3 = sb("mk3", [3, NB * P], U8)
        mk_rows = sb("mk_rows", [3, NB * P], BF16)
        mq_i = sb("mq_i", [NB, P], I32)
        mq_f = sb("mq_f", [NB, 3, P])
        mq_b = sb("mq_b", [NB, 3, P], BF16)
        c_rows = sb("c_rows", [3, NB * P], BF16)
        YT = sb("YT", [P, 2, NH, P])
        VZ = YT
        nat1 = YT[:, 0, :, :].rearrange("p (i k) s -> p i (k s)", i=2)
        qkT = YT[:, 1, :, :].rearrange("p (i k) s -> p i k s", i=2)
        A = sb("A", [P, NH, P])
        wv1 = sb("wv1", [P, INNER])
        wout = sb("wout", [P, PAIRS, P])
        gw = sb("gw", [P, NE])
        w1 = sb("w1", [P, NE, HC * P])
        w2 = sb("w2", [P, NE, HC, P])
        f1 = sb("f1", [P, HC * P])
        f2 = sb("f2", [P, HC, P])
        fb1 = sb("fb1", [P, HC])
        stats = sb("stats", [P, 3, 6])
        mv = sb("mv", [P, 3, 2])
        veps = sb("veps", [P, 3, 1])
        rstd = sb("rstd", [P, 3, 1])
        XN = sb("XN", [P, 2, P])
        CX = sb("CX", [P, 2, P])
        XCT = sb("XCT", [P, 2, 2, P])
        QF = sb("QF", [P, 2, NU, P])
        HF = sb("HF", [P, 2, NU, P])
        QS = sb("QS", [P, 2, NU, P], FP32R)
        KS = sb("KS", [P, NU, P], FP32R)
        KBD = sb("KBD", [P, 2, NU, G, P], FP32R)
        wide = sb("wide", [P, 2 * 2 * PAIRS, P])
        XK = wide[:, 0:2, :]
        V1 = wide[:, 0:2 * PAIRS, :].rearrange("p (a k) s -> p a (k s)", a=2).rearrange("p a (h d) -> p a h d", h=NH)
        OT = wide[:, 2 * PAIRS:, :].rearrange("p (a k) s -> p a k s", a=2)
        OT0 = sb("OT0", [P, 2, P])
        nmx = sb("nmx", [P, 2, NH])
        den = sb("den", [P, 2, NH])
        rden = sb("rden", [P, 2, NH])
        PR = sb("PR", [P, NU, G * P])
        PT = sb("PT", [P, 2, G * P])
        XND = sb("XND", [P, P])
        XDT = sb("XDT", [P, P])
        H = sb("H", [P, 2, HC, P])
        lgs = sb("lgs", [P, NE])
        top8 = sb("top8", [P, 8])
        topi = sb("topi", [P, 8], U32)
        hot1 = sb("hot1", [P, 2, NE])
        chosen = sb("chosen", [P, NE], BF16)
        next_row = sb("next_row", [P, NE])
        place = sb("place", [P, NE])
        picked = sb("picked", [P, 2, NE])
        scat_idx = sb("scat_idx", [P, 2, 2], U32)
        route = [HF[:].rearrange("p a g s -> p (a g s)").rearrange("p (w n e) -> p w n e", w=4, n=NB)[:, w]
                 for w in range(4)]
        topv = sb("topv", [P, 2, NB])
        tope = sb("tope", [P, 2, NB])
        gap = sb("gap", [P, NB])
        egap = sb("egap", [P, NB])
        gate = sb("gate", [P, 2, NB])
        tiles = sb("tiles", [P, 4, NE + 1])
        tile_start = sb("tile_start", [P, NE + 1], I32)
        fill_row = sb("fill_row", [P, NE], I32)
        row_shift = sb("row_shift", [P, NE], I32)
        slot_f = sb("slot_f", [P, 2, NB])
        slot = sb("slot", [P, 2, NB], U32)
        XL, XT, YB = (PR[:, k, 0:TILE].rearrange("p (h s) -> p h s", h=2) for k in range(3))
        gidx = sb("gidx", [P, 2, 2], U32)
        GY = QF[:, 0, :, :].rearrange("p (a i) s -> p a i s", a=2)
        acc = QF[:, 1, 0:2, :]

        ld_setup, ld_w0, ld_w1, ld_ffn, ld_x = (sem(s) for s in ("ld_setup", "ld_w0", "ld_w1", "ld_ffn", "ld_x"))
        const_ready, pool_self, dve_self = (sem(s) for s in ("const_ready", "pool_self", "dve_self"))
        set_pe, set_copy, rows_moved, bd_zeroed = (sem(s) for s in ("set_pe", "set_copy", "rows_moved", "bd_zeroed"))
        c_ready, c_stored, c_loaded = (sem(s) for s in ("c_ready", "c_stored", "c_loaded"))
        parts_ready, out_stored = sem("parts_ready"), [sem("out_stored0"), sem("out_stored1")]

        def wait_apart(engine, *counts):
            counts = [(s, v if isinstance(v, int) else engine.to_reg(v)) for s, v in counts]
            engine.wait_ge(const_ready, 1)
            for s, v in counts:
                wait(engine, s, v)

        def names(prefix, words):
            return {w: sem(f"{prefix}_{w}") for w in words.split()}

        common = "stat var veps rstd xn ctx0 ctx1 tr xct "
        a = names("a", common + "q k v0 qf kf hq hk vc qs bd ks s mx e rd nm t pt0 pt1 pv oT o x")
        c = names("c", common + "v vc y yc s mx e rd nm t pt0 pt1 pv oT o x")
        rt = names("rt", "stat var veps rstd xn kept tr xct lg lgc top8 topi tope hot chosen cnt place next picked slots "
                         "placed sc0 sc1 zeroed tiles final gap egap")
        b = names("b", "xl tr xt h0 h1 hr0 hr1 y0 y1 yc0 yc1 st")
        mix = names("mix", "idx g0 g1 first done")
        d = names("d", "stat var veps rstd xn tr xct h hr y x")

        block = ctx.enter_context(nc.Block())
        x_v = x.rearrange("b s d -> s b d")
        flat_mask = mask_keys.rearrange("b s -> (b s)")

        def norm_dve_stats(dve, s, prev_x, m, p):
            if prev_x is not None:
                wait(dve, prev_x, m + 1)
            nc.vector.bn_stats(stats[:, p, :], X[:, m, :]).then_inc(s["stat"], 1)
            wait_apart(dve, (s["stat"], m + 1), (s["rstd"], m - 1))
            nc.vector.bn_aggr(mv[:, p, :], stats[:, p, :]).then_inc(s["var"], 1)

        def norm_pool(pool, s, m, p):
            p = 2 if s is d or s is rt else p
            wait_apart(pool, (s["var"], m + 1))
            nc.gpsimd.tensor_scalar(veps[:, p, :], mv[:, p, 1:2], EPS, None, ALU.add).then_inc(s["veps"], 1)
            wait(pool, s["veps"], m + 1)
            wait(pool, s["xn"], m if s is d or s is rt else m - 1)
            nc.gpsimd.tensor_tensor(rstd[:, p, :], veps[:, p, :], expo[:], ALU.pow).then_inc(s["rstd"], 1)

        def norm_dve_apply(dve, s, m, p):
            wait(dve, s["rstd"], m + 1)
            wait(dve, s["tr"], m - 1)
            nc.vector.tensor_scalar(XN[:, p, :], X[:, m, :], mv[:, p, 0:1], rstd[:, p, :],
                                    ALU.subtract, ALU.mult).then_inc(s["xn"], 1)

        def norm_alone_stats(dve, s, prev, m):
            wait_apart(dve, (prev, m + 1))
            nc.vector.bn_stats(stats[:, 2, :], X[:, bass.ds(m, 1), :].rearrange("p o d -> p (o d)")).then_inc(s["stat"], 1)
            wait_apart(dve, (s["stat"], m + 1), (s["rstd"], m))
            nc.vector.bn_aggr(mv[:, 2, :], stats[:, 2, :]).then_inc(s["var"], 1)

        def norm_alone_apply(dve, s, m):
            wait(dve, s["rstd"], m + 1)
            wait(dve, s["tr"], m)
            if s is rt:
                wait(dve, s["kept"], m)
            nc.vector.tensor_scalar(XND[:], X[:, bass.ds(m, 1), :].rearrange("p o d -> p (o d)"), mv[:, 2, 0:1],
                                    rstd[:, 2, :], ALU.subtract, ALU.mult).then_inc(s["xn"], 1)

        def load_ctx(sp, s, m, p):
            wait(sp, s["tr"], m - 1)
            sp.dma_start(CX[:, p, :], ctx_in[m]).then_inc(s[f"ctx{p}"], 16)

        def scale_pool(pool, s, m, p, g):
            wait(pool, s["rd"], NU * m + g + 1)
            unit = PR[:, g, :].rearrange("p (j k) -> p j k", j=G)
            nc.gpsimd.tensor_tensor(unit, unit, rden[:, p, G * g:G * g + G].unsqueeze(2).broadcast_to([P, G, P]),
                                    ALU.mult).then_inc(s["nm"], 1)

        def diagonal(p):
            first = VZ[:, p, :, 0:DH0]
            (row, (step, count), inner) = first.ap
            return bass.AP(first.tensor, first.offset, [row, [step + DH0, count], inner])

        def scaled_units(n, p):
            return [(n - 1, 1 - p, NU - 1)] + [(n, p, g) for g in range(NU - 1)]

        def slots(n, p):
            q = 1 - p
            return [((n, p, k), (n - 1, q, k + 2) if k < 2 else (n, p, k - 2), (n - 1, q, k + 1) if k < 3 else (n, p, 0))
                    for k in range(NU)]

        @block.sync
        def _(sp):
            for src, i in ((wq0, 0), (wk0, 1), (wv0, 2), (wo0, 3)):
                sp.dma_start(nat0[:, i, :], src).then_inc(ld_w0, 16)
            sp.dma_start(mq_i[:], mask_queries).then_inc(ld_setup, 16)
            sp.dma_start(mk_bc[:], flat_mask.partition_broadcast(P)).then_inc(ld_setup, 16)
            sp.dma_start(mk3[:], flat_mask.partition_broadcast(3)).then_inc(ld_setup, 16)
            for i, src in enumerate((bv0, bo0, bout1, ffn_b2)):
                sp.dma_start(brow_f[0:1, i, 0, :], src.unsqueeze(0)).then_inc(ld_setup, 16)
            for j in range(G):
                for r in range(REPS):
                    rows = slice((j * REPS + r) * DH0, (j * REPS + r + 1) * DH0)
                    for i, src in enumerate((bq0, bk0)):
                        sp.dma_start(bqk[rows, i, :], src.rearrange("(g j d) -> j d g", g=NU, j=G)[j]).then_inc(ld_setup, 16)
            for k in range(4):
                sp.dma_start(X[:, 8 * k:8 * k + 8, :], x_v[:, 8 * k:8 * k + 8, :]).then_inc(ld_x, 16)
            sp.wait_ge(parts_ready, 1)
            for r in range(3):
                sp.dma_start(brow[r:r + 1, :, :], brow_b[0:1, :, r, :]).then_inc(rows_moved, 16)

            def step0(n, p):
                if exists(n + 2):
                    load_ctx(sp, a, n + 2, p)
                if exists(n + 1):
                    m = n + 1
                    wait_apart(sp, (a["ks"], m + 1), (a["s"], NU * (m - 1)))
                    for j in range(G):
                        rows = slice(j * REPS * DH0, (j + 1) * REPS * DH0)
                        sp.dma_start(KBD[rows, 1 - p, :, j, :].bitcast(FP32), KS[rows, :, :].bitcast(FP32)).then_inc(a["bd"], 16)

            sp.wait_ge(bd_zeroed, 1)
            sp.dma_start(ys[2 * NB * P:, :].rearrange("(k p) d -> p k d", p=P),
                         zero[:].unsqueeze(1).broadcast_to([P, 2 * NE, P])).then_inc(rt["zeroed"], 16)
            over_steps(sp, step0, -2, NB, 2)

            sp.wait_ge(c_ready, 1)
            sp.dma_start(c_dram, mq_b[:]).then_inc(c_stored, 16)
            sp.wait_ge(c_stored, 16)
            sp.dma_start(c_rows[:].rearrange("r (b s) -> r b s", b=NB), c_dram.rearrange("b r s -> r b s")).then_inc(c_loaded, 16)

            sp.wait_ge(rt["tiles"], 1)
            starts = [sp.value_load(tile_start[0:1, e:e + 1], min_val=0, max_val=MAX_TILES) for e in range(NE + 1)]
            for e in range(NE):
                fill = sp.value_load(fill_row[0:1, e:e + 1], min_val=e * REGION, max_val=e * REGION + NB * P)
                sp.dma_start(xs[bass.ds(fill, TILE), :].rearrange("(k p) d -> p k d", p=P),
                             zero[:].unsqueeze(1).broadcast_to([P, 2, P])).then_inc(rt["zeroed"], 16)
            sp.wait_ge(rt["sc0"], NB * 16)
            sp.wait_ge(rt["sc1"], NB * 16)
            sp.wait_ge(rt["zeroed"], (NE + 1) * 16)
            for e in range(NE):
                shift = sp.value_load(row_shift[0:1, e:e + 1], min_val=0, max_val=e * REGION)
                with sp.Fori(starts[e], starts[e + 1]) as t:
                    row = nc.s_assert_within(t * TILE + shift, e * REGION, e * REGION + NB * P)
                    wait_apart(sp, (b["tr"], t))
                    sp.dma_start(XL, xs[bass.ds(row, TILE), :].rearrange("(p h) d -> p h d", h=2)).then_inc(b["xl"], 16)
            total = starts[NE]
            wait_apart(sp, (b["tr"], total))
            sp.dma_start(XL, xs[0:TILE, :].rearrange("(p h) d -> p h d", h=2)).then_inc(b["xl"], 16)
            wait_apart(sp, (b["xl"], total * 16 + 16))

            def step1(n, p):
                if exists(n + 2):
                    load_ctx(sp, c, n + 2, p)
                if exists(n - 2):
                    wait(sp, d["x"], n - 1)
                    sp.dma_start(out[n - 2], acc[:, p, :]).then_inc(out_stored[p], 16)
            over_steps(sp, step1, -2, NB + 1, 3)
            sp.wait_ge(out_stored[0], 8 * NB)
            sp.wait_ge(out_stored[1], 8 * NB)

        @block.gpsimd
        def _(pool):
            nc.gpsimd.memset(ident[:], 0.0).then_inc(pool_self, 1)
            nc.gpsimd.memset(ones_row[:], 1.0)
            nc.gpsimd.memset(ones3[:], 1.0)
            nc.gpsimd.memset(expo[:], -0.5)
            nc.gpsimd.iota(iota_e[:], [[1, NE]], base=0, channel_multiplier=0, allow_small_or_imprecise_dtypes=True)
            nc.gpsimd.iota(iota_t[:], [[TILE, NB - 1]], base=TILE, channel_multiplier=0, allow_small_or_imprecise_dtypes=True)
            nc.gpsimd.memset(onesb[:], 1.0)
            nc.gpsimd.memset(upper[:], 1.0).then_inc(pool_self, 1)
            nc.gpsimd.memset(zero[:], 0.0)
            nc.gpsimd.iota(next_row[:], [[REGION, NE]], base=0, channel_multiplier=0, allow_small_or_imprecise_dtypes=True)
            nc.gpsimd.iota(region[:], [[REGION, NE]], base=0, channel_multiplier=0, allow_small_or_imprecise_dtypes=True)
            for k in range(3):
                nc.gpsimd.memset(patt[0:1, 4, k:k + 1], bf16_parts(FILL0)[k])
            nc.gpsimd.memset(patt[0:1, 4, 3:], 0.0)
            for k, low in ((0, (2, 3)), (1, (1, 3))):
                row = patt[0:1, 2 * k:2 * k + 2, :].rearrange("o k (j r d) -> o k j r d", j=G, r=REPS)
                for r in range(REPS):
                    nc.gpsimd.memset(row[:, 0, :, r, :], -1.0 if r in low else 1.0)
                    nc.gpsimd.memset(row[:, 1, :, r, :], 1.0 if r in low else 0.0)
            pool.wait_ge(pool_self, 2)
            nc.gpsimd.affine_select(out=upper[:], in_=upper[:], compare_op=ALU.is_gt, fill=0.0, base=0,
                                    pattern=[[1, P]], channel_multiplier=-1).then_inc(pool_self, 1)
            nc.gpsimd.affine_select(out=ident[:], in_=ident[:], compare_op=ALU.not_equal, fill=1.0, base=0,
                                    pattern=[[-1, P]], channel_multiplier=1).then_inc(pool_self, 1)
            pool.wait_ge(pool_self, 4)
            nc.gpsimd.memset(one1[:], 1.0).then_inc(const_ready, 1)
            nc.gpsimd.memset(KBD[:].rearrange("p a g j s -> p (a g j s)").bitcast(FP32), 0.0).then_inc(bd_zeroed, 1)

            def step0(n, p):
                for k, (m, r, g) in enumerate(scaled_units(n, p)):
                    if exists(m):
                        scale_pool(pool, a, m, r, g)
                    if k == 0 and exists(n - 2):
                        norm_pool(pool, rt, n - 2, p)
                    if k == 0 and exists(n + 2):
                        norm_pool(pool, a, n + 2, p)
                    if k in (1, 2) and exists(n - 4):
                        wait_apart(pool, (rt["placed"], n - 3), (rt["kept"], n - 3))
                        nc.gpsimd.indirect_dma_start(xs, bass.IndirectOffsetOnAxis(scat_idx[:, p, k - 1:k], 0), XK[:, p, :],
                                                     None).then_inc(rt[f"sc{p}"], 16)
                    if k == 3 and exists(n - 2):
                        wait_apart(pool, (rt["xn"], n - 1), *([(rt[f"sc{p}"], 2 * loads(n - 4, p))] if exists(n - 4) else []))
                        nc.gpsimd.tensor_copy(XK[:, p, :], XND[:]).then_inc(rt["kept"], 1)
            over_steps(pool, step0, -2, NB + 3, 2, 4)

            pool.wait_ge(rt["tiles"], 1)
            total = pool.value_load(tile_start[0:1, NE:NE + 1], min_val=NE, max_val=MAX_TILES)
            pool.wait_ge(rt["zeroed"], (NE + 1) * 16)
            with pool.Fori(0, total) as t:
                wait_apart(pool, (b["yc0"], t + 1), (b["yc1"], t + 1))
                pool.dma_start(ys[bass.ds(t * TILE, TILE), :].rearrange("(p h) d -> p h d", h=2), YB).then_inc(b["st"], 16)
            pool.wait_ge(rt["final"], 1)
            wait_apart(pool, (b["st"], total * 16))

            def step1(n, p):
                for k, (m, r, g) in enumerate(scaled_units(n, p)):
                    if exists(m):
                        scale_pool(pool, c, m, r, g)
                    if k == 0 and exists(n - 2):
                        norm_pool(pool, d, n - 2, p)
                    if k == 1 and exists(n + 2):
                        norm_pool(pool, c, n + 2, p)
                    if k == 2 and exists(n + 3):
                        g = n + 3
                        wait_apart(pool, (mix["done"], g - 1))
                        nc.gpsimd.tensor_copy(gidx[:, 1 - p, :].unsqueeze(2), slot[:, :, bass.ds(g, 1)]).then_inc(mix["idx"], 1)
                        wait_apart(pool, (mix["idx"], g + 1))
                        for i in range(2):
                            nc.gpsimd.indirect_dma_start(GY[:, 1 - p, i, :], None, ys,
                                                         bass.IndirectOffsetOnAxis(gidx[:, 1 - p, i:i + 1], 0)).then_inc(mix[f"g{1 - p}"], 16)
            over_steps(pool, step1, -3, NB + 1, 3)

        @block.scalar
        def _(act):
            for t, src in ((nat1[:, 0, :], wq1), (nat1[:, 1, :], wkv1[:, 0:INNER]), (wv1[:], wkv1[:, INNER:]),
                           (gw[:], gate_w), (wout[:], wout1.rearrange("(c p) d -> p c d", p=P))):
                act.dma_start(t, src).then_inc(ld_w1, 16)
            for t, src in ((w1[:], moe_w1.rearrange("e d h -> d e h")),
                           (w2[:], moe_w2.rearrange("e (c p) d -> p e c d", p=P)), (f1[:], ffn_w1),
                           (f2[:], ffn_w2.rearrange("(c p) d -> p c d", p=P)), (fb1[:], ffn_b1.rearrange("(c p) -> p c", p=P))):
                act.dma_start(t, src).then_inc(ld_ffn, 16)

            def read_xct(s, m, p, both, free_sem, free_count):
                M_BANK = M2_BANK if s is a else bank[7]
                act.wait_ge(s["tr"], m + 1)
                wait(act, free_sem, free_count)
                k = 2 if both else 1
                nc.scalar.activation(XCT[:, p, 0:k, :], M_BANK[:, 0:k * P].rearrange("p (k s) -> p k s", k=k),
                                     ACT.Copy).then_inc(s["xct"], 1)

            def exponentials(s, m, p, g):
                wait_apart(act, (s["mx"], NU * m + g + 1), (s["t"], NU * (m - 1) + g + 1))
                for j in range(G):
                    h = G * g + j
                    last = nc.scalar.activation(PR[:, g, j * P:(j + 1) * P], S_BANK[g % 2][:, j * P:(j + 1) * P], ACT.Exp,
                                                bias=nmx[:, p, h:h + 1], accum_out=den[:, p, h:h + 1])
                last.then_inc(s["e"], 1)

            def read_PT(s, m, g):
                act.wait_ge(s["t"], NU * m + g + 1)
                wait(act, s["pv"], NU * m + g - 1)
                nc.scalar.activation(PT[:, g % 2, :], T_BANK[g % 2][:], ACT.Copy).then_inc(s["pt1"], 1)

            def step0(n, p):
                q, m = 1 - p, n + 1
                if exists(m):
                    read_xct(a, m, q, True, a["v0"], m - 1)
                if exists(n):
                    exponentials(a, n, p, 0)
                    exponentials(a, n, p, 1)
                if exists(n - 1):
                    read_PT(a, n - 1, 3)
                if exists(m):
                    act.wait_ge(a["q"], m + 1)
                    wait(act, a["qs"], m)
                    for g in range(NU):
                        last = nc.scalar.activation(QF[:, 0, g, :], bank[4][:, g * P:(g + 1) * P], ACT.Identity,
                                                    bias=bqk[:, 0, g:g + 1], scale=float(DH0) ** -0.5)
                    last.then_inc(a["qf"], 1)
                    act.wait_ge(a["qf"], m + 1)
                    nc.scalar.activation(HF[:, 0, :, :].bitcast(FP32R), QF[:, 0, :, :], ACT.Copy,
                                         scale=pcol[:, 0:1]).then_inc(a["hq"], 1)
                if exists(n - 1):
                    act.wait_ge(a["pv"], NU * n)
                    wait(act, a["o"], n - 2)
                    nc.scalar.activation(OT0[:, q, :], bank[6][:, 0:P], ACT.Copy).then_inc(a["oT"], 1)
                if exists(n):
                    exponentials(a, n, p, 2)
                if exists(n):
                    exponentials(a, n, p, 3)
                    read_PT(a, n, 1)
                if exists(m):
                    act.wait_ge(a["v0"], m + 1)
                    wait(act, a["pv"], NU * (m - 1))
                    nc.scalar.activation(diagonal(q), M_BANK[:, 0:P].rearrange("p (h d) -> p h d", h=NH),
                                         ACT.Copy).then_inc(a["vc"], 1)
            over_steps(act, step0, -2, NB, 2)

            act.wait_ge(rt["gap"], 1)
            nc.scalar.activation(egap[:], gap[:], ACT.Exp).then_inc(rt["egap"], 1)

            act.wait_ge(rt["tiles"], 1)
            total = act.value_load(tile_start[0:1, NE:NE + 1], min_val=NE, max_val=MAX_TILES)
            with act.Fori(0, total) as t:
                for k in range(2):
                    act.wait_ge(b[f"h{k}"], t + 1)
                    act.wait_ge(b[f"y{k}"], t)
                    nc.scalar.activation(H[:, k, :, :].rearrange("p c s -> p (c s)"), bank[k][:], ACT.Relu).then_inc(b[f"hr{k}"], 1)

            def step1(n, p):
                q, m = 1 - p, n + 1

                def read_v(half):
                    act.wait_ge(c["v"], 2 * m + half + 1)
                    wait(act, c["pv"], NU * (m - 1))
                    nc.scalar.activation(V1[:, q, 8 * half:8 * half + 8, :], bank[4][:].rearrange("p (h d) -> p h d", h=8),
                                         ACT.Copy).then_inc(c["vc"], 1)

                def read_heads(half):
                    act.wait_ge(c["pv"], NU * (n - 1) + 2 * half + 2)
                    wait(act, c["o"], n - 2)
                    nc.scalar.activation(OT[:, q, 4 * half:4 * half + 4, :].rearrange("p c s -> p (c s)"), bank[5 + half][:],
                                         ACT.Copy).then_inc(c["oT"], 1)

                if exists(m):
                    read_xct(c, m, q, True, c["s"], NU * (m - 1))
                if exists(n):
                    exponentials(c, n, p, 0)
                if exists(n - 1):
                    read_heads(0)
                if exists(n):
                    exponentials(c, n, p, 1)
                if exists(n - 1):
                    read_PT(c, n - 1, 3)
                if exists(n):
                    exponentials(c, n, p, 2)
                if exists(n - 1):
                    read_heads(1)
                if exists(n):
                    exponentials(c, n, p, 3)
                if exists(m):
                    read_v(0)
                if exists(n):
                    read_PT(c, n, 1)
                if exists(m):
                    read_v(1)
            over_steps(act, step1, -2, NB + 1, 3)

        @block.vector
        def _(dve):
            chain = [0]

            def link(ins):
                chain[0] += 1
                ins.then_inc(dve_self, 1)
                dve.wait_ge(dve_self, chain[0])

            dve.wait_ge(set_pe, 2)
            for i in range(2):
                src = bank[1][:, i * P:(i + 1) * P].rearrange("p (g j d) -> p g j d", g=NU, j=G)
                dst = wqk_rep[:, i, :, :].rearrange("p g (j r d) -> p g j r d", j=G, r=REPS)
                for r in range(REPS):
                    for g in range(NU):
                        nc.vector.tensor_copy(dst[:, g, :, r, :], src[:, g, :, :])
            nc.vector.tensor_copy(wv0T[:], bank[1][:, 2 * P:3 * P])
            nc.vector.tensor_copy(wo0T[:], bank[1][:, 3 * P:4 * P])
            nc.vector.memset(den[:, 0, :], 0.0).then_inc(set_copy, 1)
            for t in range(2 * PAIRS // 4):
                dve.wait_ge(set_pe, 3 + t)
                i, k = t // 2, 4 * (t % 2)
                nc.vector.tensor_copy(qkT[:, i, k:k + 4, :].rearrange("p c s -> p (c s)"), bank[2 + t % 2][:]).then_inc(set_copy, 1)
            for g in range(NU):
                dve.wait_ge(set_pe, 7 + g)
                even_odd = A[:, 8 * (g // 2):8 * (g // 2) + 8, :].rearrange("p (j o) s -> p o j s", o=2)
                nc.vector.tensor_scalar(even_odd[:, g % 2], bank[2 + g % 2][:].rearrange("p (j s) -> p j s", j=G),
                                        float(DH1) ** -0.5, None, ALU.mult).then_inc(set_copy, 1)
            SETUP_COPIES = 1 + 4 + NU
            dve.wait_ge(set_copy, SETUP_COPIES)
            link(nc.vector.memset(VZ[:], 0.0))
            dve.wait_ge(ld_setup, 16 * (5 + 2 * G * REPS + 2))
            link(nc.vector.tensor_copy(brow_b[:, :, 0, :], brow_f[:, 0:4, 0, :]))
            link(nc.vector.tensor_tensor(brow_f[:, 0:4, 1, :], brow_f[:, 0:4, 0, :], brow_b[:, :, 0, :], ALU.subtract))
            link(nc.vector.tensor_copy(brow_b[:, :, 1, :], brow_f[:, 0:4, 1, :]))
            nc.vector.tensor_tensor(brow_b[:, :, 2, :], brow_f[:, 0:4, 1, :], brow_b[:, :, 1, :],
                                    ALU.subtract).then_inc(parts_ready, 1)
            link(nc.vector.tensor_scalar(mq_f[:, 0, :], mq_i[:], -1.0, 1.0, ALU.mult, ALU.add))
            link(nc.vector.tensor_scalar(mq_f[:, 1, :], mq_f[:, 0, :], -FILL1, None, ALU.mult))
            link(nc.vector.tensor_copy(mq_b[:, 0, :], mq_f[:, 1, :]))
            link(nc.vector.tensor_tensor(mq_f[:, 2, :], mq_f[:, 1, :], mq_b[:, 0, :], ALU.subtract))
            link(nc.vector.tensor_copy(mq_b[:, 1, :], mq_f[:, 2, :]))
            nc.vector.tensor_tensor(mq_b[:, 2, :], mq_f[:, 2, :], mq_b[:, 1, :], ALU.subtract).then_inc(c_ready, 1)
            dve.wait_ge(set_pe, 1)
            link(nc.vector.tensor_copy(pcol[:], bank[0][:, 0:5]))
            nc.vector.tensor_scalar(mk_rows[:], mk3[:], -1.0, pcol[0:3, 4:5], ALU.add, ALU.mult)
            link(nc.vector.tensor_scalar(bqk[:, 0, :], bqk[:, 0, :], float(DH0) ** -0.5, None, ALU.mult))
            dve.wait_ge(ld_x, 64)

            def row_max(s, m, p, g):
                dve.wait_ge(s["s"], NU * m + g + 1)
                nc.vector.tensor_reduce(nmx[:, p, G * g:G * g + G], S_BANK[g % 2][:].rearrange("p (j k) -> p j k", j=G),
                                        AXX, ALU.max, negate=True).then_inc(s["mx"], 1)

            def sums_reciprocal(s, m, p, g):
                dve.wait_ge(s["e"], NU * m + g + 1)
                nc.vector.reciprocal(rden[:, p, G * g:G * g + G], den[:, p, G * g:G * g + G]).then_inc(s["rd"], 1)

            def read_PT(s, m, g):
                dve.wait_ge(s["t"], NU * m + g + 1)
                wait(dve, s["pv"], NU * m + g - 1)
                nc.vector.tensor_copy(PT[:, g % 2, :], T_BANK[g % 2][:]).then_inc(s["pt0"], 1)

            def step0(n, p):
                q, m = 1 - p, n + 1
                if exists(n):
                    row_max(a, n, p, 0)
                if exists(n - 1):
                    sums_reciprocal(a, n - 1, q, 3)
                if exists(n - 1):
                    read_PT(a, n - 1, 2)
                if exists(n - 4):
                    dve.wait_ge(rt["cnt"], n - 3)
                    nc.vector.tensor_tensor(place[:], M_BANK[:, 0:NE], next_row[:], ALU.add).then_inc(rt["place"], 1)
                    wait(dve, rt["place"], n - 3)
                    nc.vector.tensor_tensor(next_row[:], M_BANK[:, NE:2 * NE], next_row[:], ALU.add).then_inc(rt["next"], 1)
                    nc.vector.tensor_tensor(picked[:], hot1[:], place[:].unsqueeze(1).broadcast_to([P, 2, NE]),
                                            ALU.mult).then_inc(rt["picked"], 1)
                if exists(n - 2):
                    norm_alone_stats(dve, rt, a["x"], n - 2)
                if exists(n + 2):
                    norm_dve_stats(dve, a, None, n + 2, p)
                if exists(m):
                    dve.wait_ge(a["k"], m + 1)
                    for g in range(NU):
                        last = nc.vector.scalar_tensor_tensor(QF[:, 1, g, :], bank[4][:, g * P:(g + 1) * P],
                                                              bqk[:, 1, g:g + 1], mk_bc[:, bass.ds(m * P, P)],
                                                              ALU.add, ALU.mult)
                    last.then_inc(a["kf"], 1)
                if exists(n):
                    row_max(a, n, p, 1)
                    sums_reciprocal(a, n, p, 0)
                if exists(m):
                    dve.wait_ge(a["kf"], m + 1)
                    nc.vector.tensor_scalar(HF[:, 1, :, :].bitcast(FP32R), QF[:, 1, :, :], pcol[:, 2:3], None,
                                            ALU.mult).then_inc(a["hk"], 1)
                    dve.wait_ge(a["hk"], m + 1)
                    wait(dve, a["bd"], 16 * G * m)
                    nc.vector.scalar_tensor_tensor(KS[:], QF[:, 1, :, :], pcol[:, 3:4], HF[:, 1, :, :],
                                                   ALU.mult, ALU.add).then_inc(a["ks"], 1)
                if exists(n):
                    row_max(a, n, p, 2)
                if exists(n - 3):
                    dve.wait_ge(rt["lg"], n - 2)
                    nc.vector.tensor_copy(lgs[:], M_BANK[:, 0:NE]).then_inc(rt["lgc"], 1)
                if exists(n - 4):
                    wait(dve, rt["picked"], n - 3)
                    nc.vector.tensor_reduce(slot_f[:, :, bass.ds(n - 4, 1)].rearrange("p k o -> p (k o)"), picked[:], AXX,
                                            ALU.add).then_inc(rt["slots"], 1)
                if exists(n - 3):
                    wait_apart(dve, (rt["lgc"], n - 2))
                    nc.vector.max(top8[:], lgs[:]).then_inc(rt["top8"], 1)
                if exists(n - 4):
                    wait_apart(dve, (rt["slots"], n - 3), (rt[f"sc{p}"], 2 * loads(n - 6, p) if exists(n - 6) else 0))
                    nc.vector.tensor_copy(scat_idx[:, p, :].unsqueeze(2), slot_f[:, :, bass.ds(n - 4, 1)]).then_inc(rt["placed"], 1)
                if exists(n - 3):
                    wait_apart(dve, (rt["top8"], n - 2))
                    nc.vector.max_index(topi[:], top8[:], lgs[:]).then_inc(rt["topi"], 1)
                    nc.vector.tensor_copy(topv[:, :, bass.ds(n - 3, 1)], top8[:, 0:2].unsqueeze(2))
                if exists(n - 2):
                    norm_alone_apply(dve, rt, n - 2)
                if exists(n - 3):
                    wait_apart(dve, (rt["topi"], n - 2))
                    nc.vector.tensor_copy(tope[:, :, bass.ds(n - 3, 1)], topi[:, 0:2].unsqueeze(2)).then_inc(rt["tope"], 1)
                if exists(n):
                    sums_reciprocal(a, n, p, 1)
                if exists(n - 3):
                    wait(dve, rt["tope"], n - 2)
                    nc.vector.tensor_tensor(hot1[:], iota_e[:].unsqueeze(1).broadcast_to([P, 2, NE]),
                                            tope[:, :, bass.ds(n - 3, 1)].broadcast_to([P, 2, NE]), ALU.is_equal).then_inc(rt["hot"], 1)
                if exists(n):
                    read_PT(a, n, 0)
                if exists(n - 3):
                    wait(dve, rt["hot"], n - 2)
                    wait(dve, rt["cnt"], n - 3)
                    nc.vector.tensor_tensor(chosen[:], hot1[:, 0, :], hot1[:, 1, :], ALU.add).then_inc(rt["chosen"], 1)
                if exists(n - 2):
                    dve.wait_ge(rt["tr"], n - 1)
                    wait(dve, rt["lg"], n - 2)
                    nc.vector.tensor_copy(XDT[:], M_BANK[:, 0:P]).then_inc(rt["xct"], 1)
                if exists(m):
                    dve.wait_ge(a["hq"], m + 1)
                    wait(dve, a["s"], NU * (m - 1))
                    nc.vector.scalar_tensor_tensor(QS[:, q, :, :], QF[:, 0, :, :], pcol[:, 1:2], HF[:, 0, :, :],
                                                   ALU.mult, ALU.add).then_inc(a["qs"], 1)
                if exists(n):
                    row_max(a, n, p, 3)
                    sums_reciprocal(a, n, p, 2)
                if exists(n + 2):
                    norm_dve_apply(dve, a, n + 2, p)
                if exists(n - 1):
                    dve.wait_ge(a["o"], n)
                    xrow = X[:, bass.ds(n - 1, 1), :].rearrange("p o d -> p (o d)")
                    nc.vector.tensor_tensor(xrow, M2_BANK[:, 0:P], xrow, ALU.add).then_inc(a["x"], 1)
            over_steps(dve, step0, -2, NB + 3, 2, 4)

            dve.wait_ge(rt["slots"], NB)
            dve.wait_ge(rt["next"], NB)
            dve.wait_ge(a["x"], NB)
            e_axis = iota_e[:].unsqueeze(1).broadcast_to([P, NB, NE])
            nc.vector.tensor_copy(fill_row[:], next_row[:])
            nc.vector.tensor_tensor(gap[:], topv[:, 1, :], topv[:, 0, :], ALU.subtract).then_inc(rt["gap"], 1)
            link(nc.vector.tensor_tensor(place[:], next_row[:], region[:], ALU.subtract))
            span = route[3].rearrange("p n e -> p e n")[:, :, 0:NB - 1]
            link(nc.vector.tensor_tensor(span, place[:].unsqueeze(2).broadcast_to([P, NE, NB - 1]),
                                         iota_t[:].unsqueeze(1).broadcast_to([P, NE, NB - 1]), ALU.is_gt))
            link(nc.vector.tensor_reduce(tiles[:, 0, 0:NE], span, AXX, ALU.add))
            link(nc.vector.memset(tiles[:, 1:3, :], 0.0))
            link(nc.vector.tensor_scalar(tiles[:, 1, 1:NE + 1], tiles[:, 0, 0:NE], 1.0, None, ALU.add))
            now, other, shift = 1, 2, 1
            while shift < NE + 1:
                nc.vector.tensor_copy(tiles[:, other, 0:shift], tiles[:, now, 0:shift])
                link(nc.vector.tensor_tensor(tiles[:, other, shift:], tiles[:, now, shift:], tiles[:, now, 0:NE + 1 - shift], ALU.add))
                now, other, shift = other, now, 2 * shift
            nc.vector.tensor_copy(tile_start[:], tiles[:, now, :])
            link(nc.vector.tensor_scalar(tiles[:, 3, :], tiles[:, now, :], float(TILE), None, ALU.mult))
            link(nc.vector.tensor_tensor(place[:], region[:], tiles[:, 3, 0:NE], ALU.subtract))
            nc.vector.tensor_copy(row_shift[:], place[:]).then_inc(rt["tiles"], 1)
            for k in range(2):
                link(nc.vector.tensor_tensor(route[0], e_axis, tope[:, k, :].unsqueeze(2).broadcast_to([P, NB, NE]), ALU.is_equal))
                link(nc.vector.tensor_tensor(route[1], route[0], place[:].unsqueeze(1).broadcast_to([P, NB, NE]), ALU.mult))
                link(nc.vector.tensor_reduce(route[2][:, :, k], route[1], AXX, ALU.add))
                link(nc.vector.tensor_tensor(slot_f[:, k, :], slot_f[:, k, :], route[2][:, :, k], ALU.subtract))
            nc.vector.tensor_copy(slot[:], slot_f[:]).then_inc(rt["final"], 1)
            dve.wait_ge(rt["egap"], 1)
            link(nc.vector.tensor_scalar(gap[:], egap[:], 1.0, None, ALU.add))
            link(nc.vector.reciprocal(gate[:, 0, :], gap[:]))
            link(nc.vector.tensor_tensor(gate[:, 1, :], gate[:, 0, :], egap[:], ALU.mult))

            dve.wait_ge(rt["tiles"], 1)
            total = dve.value_load(tile_start[0:1, NE:NE + 1], min_val=NE, max_val=MAX_TILES)
            dve.wait_ge(b["tr"], 1)
            nc.vector.tensor_copy(XT.rearrange("p h s -> p (h s)"), bank[2][:, 0:TILE]).then_inc(b["xt"], 1)
            with dve.Fori(0, total) as t:
                dve.wait_ge(b["tr"], t + 2)
                dve.wait_ge(b["h1"], t + 1)
                nc.vector.tensor_copy(XT.rearrange("p h s -> p (h s)"), bank[2][:, 0:TILE]).then_inc(b["xt"], 1)
                for k in range(2):
                    dve.wait_ge(b[f"y{k}"], t + 1)
                    dve.wait_ge(b["st"], t * 16)
                    nc.vector.tensor_copy(YB[:, k, :], bank[4 + k][:, 0:P]).then_inc(b[f"yc{k}"], 1)

            def step1(n, p):
                q, m = 1 - p, n + 1

                def read_y(g):
                    dve.wait_ge(c["y"], NU * m + g + 1)
                    wait(dve, c["s"], NU * (m - 1))
                    nc.vector.tensor_copy(YT[:, q, G * g:G * g + G, :].rearrange("p h s -> p (h s)"),
                                          bank[4][:]).then_inc(c["yc"], 1)

                if exists(n):
                    row_max(c, n, p, 0)
                if exists(n - 2):
                    norm_alone_stats(dve, d, c["x"], n - 2)
                if exists(n - 1):
                    sums_reciprocal(c, n - 1, q, 3)
                if exists(n + 2):
                    g = n + 2
                    dve.wait_ge(mix[f"g{p}"], 2 * loads(g, p))
                    xrow = X[:, bass.ds(g, 1), :].rearrange("p o d -> p (o d)")

                def add_experts(i, done):
                    nc.vector.scalar_tensor_tensor(xrow, GY[:, p, i, :], gate[:, i, bass.ds(n + 2, 1)], xrow,
                                                   ALU.mult, ALU.add).then_inc(mix[done], 1)

                if exists(n + 2):
                    add_experts(0, "first")
                if exists(m):
                    read_y(0)
                if exists(n + 2):
                    wait_apart(dve, (mix["first"], n + 3))
                    add_experts(1, "done")
                    wait_apart(dve, (mix["done"], n + 3))
                    norm_dve_stats(dve, c, None, n + 2, p)
                if exists(n - 1):
                    read_PT(c, n - 1, 2)
                if exists(n - 2):
                    norm_alone_apply(dve, d, n - 2)
                if exists(n):
                    row_max(c, n, p, 1)
                if exists(m):
                    read_y(1)
                if exists(n):
                    sums_reciprocal(c, n, p, 0)
                if exists(n - 2):
                    dve.wait_ge(d["tr"], n - 1)
                    wait(dve, d["h"], n - 2)
                    nc.vector.tensor_copy(XDT[:], bank[7][:, 0:P]).then_inc(d["xct"], 1)
                if exists(m):
                    read_y(2)
                if exists(n):
                    row_max(c, n, p, 2)
                if exists(n - 2):
                    dve.wait_ge(d["h"], n - 1)
                    wait(dve, d["y"], n - 2)
                    for k in range(HC):
                        last = nc.vector.tensor_scalar(H[:, 0, k, :], bank[4][:, k * P:(k + 1) * P], fb1[:, k:k + 1], 0.0,
                                                       ALU.add, ALU.max)
                    last.then_inc(d["hr"], 1)
                if exists(n):
                    sums_reciprocal(c, n, p, 1)
                    read_PT(c, n, 0)
                if exists(n):
                    row_max(c, n, p, 3)
                if exists(m):
                    read_y(3)
                if exists(n):
                    sums_reciprocal(c, n, p, 2)
                if exists(n + 2):
                    norm_dve_apply(dve, c, n + 2, p)
                if exists(n - 2):
                    dve.wait_ge(d["y"], n - 1)
                    wait(dve, out_stored[p], loads(n - 4, p))
                    nc.vector.tensor_tensor(acc[:, p, :], bank[7][:, 0:P],
                                            X[:, bass.ds(n - 2, 1), :].rearrange("p o d -> p (o d)"),
                                            ALU.add).then_inc(d["x"], 1)
                if exists(n - 1):
                    dve.wait_ge(c["o"], n)
                    xrow = X[:, bass.ds(n - 1, 1), :].rearrange("p o d -> p (o d)")
                    nc.vector.tensor_tensor(xrow, bank[7][:, 0:P], xrow, ALU.add).then_inc(c["x"], 1)
            over_steps(dve, step1, -2, NB + 1, 3)

        @block.tensor
        def _(pe):
            mm = nc.tensor.matmul
            pe.wait_ge(const_ready, 1)
            for k in range(5):
                last = mm(bank[0][:, k:k + 1], patt[0:1, k, :], one1[:], start=True, stop=True)
            last.then_inc(set_pe, 1)
            pe.wait_ge(ld_w0, 64)
            for i in range(4):
                last = nc.tensor.transpose(bank[1][:, i * P:(i + 1) * P], nat0[:, i, :], ident[:])
            last.then_inc(set_pe, 1)
            pe.wait_ge(ld_w1, 80)
            for t in range(2 * PAIRS // 4):
                i, k = t // 2, 4 * (t % 2)
                if t >= 2:
                    pe.wait_ge(set_copy, 1 + t - 1)
                for j in range(4):
                    last = nc.tensor.transpose(bank[2 + t % 2][:, j * P:(j + 1) * P], nat1[:, i, (k + j) * P:(k + j + 1) * P], ident[:])
                last.then_inc(set_pe, 1)
            for g in range(NU):
                pe.wait_ge(set_copy, 1 + 4 + max(0, g - 1))
                for j in range(G):
                    h = 8 * (g // 2) + 2 * j + g % 2
                    rows = slice(DH1 * (h % 2), DH1 * (h % 2 + 1))
                    last = mm(bank[2 + g % 2][:, j * P:(j + 1) * P], qkT[rows, 0, h // 2, :], qkT[rows, 1, h // 2, :],
                              start=True, stop=True)
                last.then_inc(set_pe, 1)
            pe.wait_ge(set_copy, 1 + 4 + NU)
            pe.wait_ge(rows_moved, 48)

            def transpose_in(s, m, p, both, m_free, m_count):
                M_BANK = M2_BANK if s is a else bank[7]
                pe.wait_ge(s["xn"], m + 1)
                if both:
                    pe.wait_ge(s[f"ctx{p}"], loads(m, p))
                wait(pe, m_free, m_count)
                last = nc.tensor.transpose(M_BANK[:, 0:P], XN[:, p, :], ident[:])
                if both:
                    last = nc.tensor.transpose(M_BANK[:, P:2 * P], CX[:, p, :], ident[:])
                last.then_inc(s["tr"], 1)

            def transpose_unit(s, m, g):
                wait(pe, s["nm"], NU * m + g + 1)
                wait(pe, s[f"pt{g % 2}"], 2 * m + g // 2)
                for j in range(G):
                    last = nc.tensor.transpose(T_BANK[g % 2][:, j * P:(j + 1) * P], PR[:, g, j * P:(j + 1) * P], ident[:])
                last.then_inc(s["t"], 1)

            def step0(n, p):
                q, m = 1 - p, n + 1

                def scores(m, p, g):
                    waits = [(a["e"], NU * m + g - 1)]
                    if g == 0:
                        waits += [(a["qs"], m + 1), (a["bd"], 16 * G * (m + 1))]
                    wait_apart(pe, *waits)
                    mm(S_BANK[g % 2][:].rearrange("p (j k) -> p j k", j=G), ones3[:],
                       mk_rows[:, bass.ds(m * P, P)].unsqueeze(1).broadcast_to([3, G, P]), start=True, stop=False,
                       skip_group_check=True)
                    mm(S_BANK[g % 2][:], QS[:, p, g, :], KBD[:, p, g, :, :].rearrange("p j s -> p (j s)"),
                       start=False, stop=True, skip_group_check=True).then_inc(a["s"], 1)

                def values(m, p, g):
                    wait(pe, a[f"pt{g % 2}"], 2 * m + g // 2 + 1)
                    if g == 0:
                        pe.wait_ge(a["vc"], m + 1)
                        wait(pe, a["oT"], m)
                    for j in range(G):
                        h = G * g + j
                        last = mm(bank[6][:, 0:P], VZ[:, p, h, :], PT[:, g % 2, j * P:(j + 1) * P],
                                  start=(h == 0), stop=(h == NH - 1))
                    last.then_inc(a["pv"], 1)

                def project(i, name, free_sem, free_count):
                    pe.wait_ge(a["xct"], m + 1)
                    wait(pe, free_sem, free_count)
                    for g in range(NU):
                        last = mm(bank[4][:, g * P:(g + 1) * P], wqk_rep[:, i, g, :], XCT[:, q, i, :], start=True, stop=True)
                    last.then_inc(a[name], 1)

                for k, (scored, turned, used) in enumerate(slots(n, p)):
                    if exists(scored[0]):
                        scores(*scored)
                    if k == 1 and exists(n - 3):
                        wait(pe, rt["xct"], n - 2)
                        wait(pe, *((rt["next"], n - 3) if exists(n - 4) else (a["vc"], min(m, NB))))
                        mm(M_BANK[:, 0:NE], XDT[:], gw[:], start=True, stop=True).then_inc(rt["lg"], 1)
                    if exists(turned[0]):
                        transpose_unit(a, turned[0], turned[2])
                    if k == 0 and exists(n - 4):
                        wait(pe, a["vc"], min(m, NB) if isinstance(n, int) else m)
                        if isinstance(n, int) and n >= NB:
                            pe.wait_ge(rt["xct"], min(n - 2, NB))
                        wait(pe, rt["lgc"], n - 3)
                        wait(pe, rt["chosen"], n - 3)
                        mm(M_BANK[:, 0:NE], upper[:], chosen[:], start=True, stop=True)
                        mm(M_BANK[:, NE:2 * NE], onesb[:], chosen[:], start=True, stop=True).then_inc(rt["cnt"], 1)
                    if k == 0 and exists(m):
                        transpose_in(a, m, q, True, *((a["xct"], m) if isinstance(n, int) and n < 2 else (a["x"], n - 1)))
                    if exists(used[0]):
                        values(*used)
                    if k == 2 and exists(n - 2):
                        wait(pe, rt["xn"], n - 1)
                        wait(pe, *((rt["lgc"], n - 2) if exists(n - 3) else (a["vc"], m)))
                        nc.tensor.transpose(M_BANK[:, 0:P], XND[:], ident[:]).then_inc(rt["tr"], 1)
                    if k == 3 and exists(m):
                        wait(pe, *((rt["xct"], n - 1) if exists(n - 2) else (a["vc"], m)))
                        mm(M_BANK[:, 0:P], XCT[:, q, 1, :], wv0T[:], start=True, stop=False)
                        mm(M_BANK[:, 0:P], ones3[:], brow[:, 0, :], start=False, stop=True).then_inc(a["v0"], 1)
                    if k == 0 and exists(m):
                        project(1, "k", a["qf"], m)
                    if k == 1 and exists(m):
                        project(0, "q", a["kf"], m + 1)
                    if k == 3 and exists(n - 1):
                        wait(pe, a["oT"], n)
                        if exists(m):
                            pe.wait_ge(a["xct"], m + 1)
                        else:
                            wait(pe, a["x"], n - 1)
                        mm(M2_BANK[:, 0:P], OT0[:, q, :], wo0T[:], start=True, stop=False)
                        mm(M2_BANK[:, 0:P], ones3[:], brow[:, 1, :], start=False, stop=True).then_inc(a["o"], 1)
            over_steps(pe, step0, -2, NB + 3, 2, 4)

            pe.wait_ge(ld_ffn, 80)

            def transpose_tile(t):
                pe.wait_ge(b["xl"], t * 16 + 16)
                for k in range(2):
                    last = nc.tensor.transpose(bank[2][:, k * P:(k + 1) * P], XL[:, k, :], ident[:])
                last.then_inc(b["tr"], 1)

            pe.wait_ge(rt["tiles"], 1)
            starts = [pe.value_load(tile_start[0:1, e:e + 1], min_val=0, max_val=MAX_TILES) for e in range(NE + 1)]
            transpose_tile(0)
            for e in range(NE):
                with pe.Fori(starts[e], starts[e + 1]) as t:
                    pe.wait_ge(b["xt"], t + 1)
                    for k in range(2):
                        pe.wait_ge(b[f"hr{k}"], t)
                        for i in range(HC):
                            last = mm(bank[k][:, i * P:(i + 1) * P], w1[:, e, i * P:(i + 1) * P], XT[:, k, :], start=True, stop=True)
                        last.then_inc(b[f"h{k}"], 1)
                    transpose_tile(t + 1)
                    for k in range(2):
                        pe.wait_ge(b[f"hr{k}"], t + 1)
                        pe.wait_ge(b[f"yc{k}"], t)
                        for i in range(HC):
                            last = mm(bank[4 + k][:, 0:P], H[:, k, i, :], w2[:, e, i, :], start=(i == 0), stop=(i == HC - 1))
                        last.then_inc(b[f"y{k}"], 1)
            total = starts[NE]

            pe.wait_ge(c_loaded, 16)
            def step1(n, p):
                q, m = 1 - p, n + 1

                def project_v(half):
                    if half:
                        pe.wait_ge(c["vc"], 2 * m + 1)
                    else:
                        pe.wait_ge(c["yc"], NU * (m + 1))
                    mm(bank[4][:], XCT[:, q, 1, :], wv1[:, 512 * half:512 * half + 512], start=True, stop=True).then_inc(c["v"], 1)

                def project_y(g):
                    if g == 0:
                        pe.wait_ge(c["xct"], m + 1)
                        wait(pe, c["vc"], 2 * m)
                    else:
                        pe.wait_ge(c["yc"], NU * m + g)
                        if g == 3 and exists(n - 2):
                            pe.wait_ge(d["hr"], n - 1)
                    for j in range(G):
                        last = mm(bank[4][:, j * P:(j + 1) * P], A[:, G * g + j, :], XCT[:, q, 0, :], start=True, stop=True)
                    last.then_inc(c["y"], 1)

                def scores(m, p, g):
                    wait(pe, c["yc"], NU * m + g + 1)
                    wait(pe, c["e"], NU * m + g - 1)
                    for j in range(G):
                        mm(S_BANK[g % 2][:, j * P:(j + 1) * P], YT[:, p, G * g + j, :], XCT[:, p, 1, :], start=(j == 0), stop=False,
                           skip_group_check=True)
                    mm(S_BANK[g % 2][:], c_rows[:, bass.ds(m * P, P)], ones_row[:], start=False, stop=True,
                       skip_group_check=True).then_inc(c["s"], 1)

                def values(m, p, g):
                    wait(pe, c[f"pt{g % 2}"], 2 * m + g // 2 + 1)
                    if g == 0:
                        pe.wait_ge(c["vc"], 2 * m + 2)
                    if g % 2 == 0:
                        wait(pe, c["oT"], 2 * (m - 1) + g // 2 + 1)
                    for j in range(G):
                        h = G * g + j
                        rows = slice(DH1 * (j % 2), DH1 * (j % 2 + 1))
                        cols = 2 * P * (g % 2) + P * (j // 2)
                        last = mm(bank[5 + g // 2][rows, cols:cols + P], V1[:, p, h, :], PT[:, g % 2, j * P:(j + 1) * P],
                                  start=True, stop=True)
                    last.then_inc(c["pv"], 1)

                for k, (scored, turned, used) in enumerate(slots(n, p)):
                    if exists(scored[0]):
                        scores(*scored)
                    if k == 0 and exists(m):
                        if is_first(n):
                            pe.wait_ge(b["yc1"], total)
                            pe.wait_ge(b["xt"], total + 1)
                        transpose_in(c, m, q, True, *((c["xct"], m) if isinstance(n, int) and n < 1 else (c["x"], n - 1)))
                    if k == 1 and exists(m):
                        project_y(1)
                    if k == 3 and exists(m):
                        project_y(3)
                    if k == 2 and exists(n - 2):
                        wait(pe, d["xct"], n - 1)
                        if exists(m):
                            pe.wait_ge(c["yc"], NU * m + 3)
                        else:
                            pe.wait_ge(c["vc"], 2 * NB)
                            pe.wait_ge(d["hr"], n - 2)
                        for kk in range(HC):
                            last = mm(bank[4][:, kk * P:(kk + 1) * P], f1[:, kk * P:(kk + 1) * P], XDT[:], start=True, stop=True)
                        last.then_inc(d["h"], 1)
                    if exists(turned[0]):
                        transpose_unit(c, turned[0], turned[2])
                    if k == 0 and exists(m):
                        project_y(0)
                    if k == 1 and exists(n - 2):
                        wait(pe, d["xn"], n - 1)
                        if exists(m):
                            pe.wait_ge(c["xct"], m + 1)
                        else:
                            wait(pe, c["x"], min(n - 1, NB))
                        nc.tensor.transpose(bank[7][:, 0:P], XND[:], ident[:]).then_inc(d["tr"], 1)
                    if k == 3 and exists(n - 2):
                        wait(pe, d["hr"], n - 1)
                        wait(pe, d["xct"], n - 1)
                        for kk in range(HC):
                            mm(bank[7][:, 0:P], H[:, 0, kk, :], f2[:, kk, :], start=(kk == 0), stop=False)
                        mm(bank[7][:, 0:P], ones3[:], brow[:, 3, :], start=False, stop=True).then_inc(d["y"], 1)
                    if k == 3 and exists(m):
                        project_v(0)
                    if exists(used[0]):
                        values(*used)
                    if k == 1 and exists(m):
                        project_y(2)
                    if k == 3 and exists(n - 1):
                        wait(pe, c["oT"], 2 * n)
                        if exists(n - 2):
                            wait(pe, d["x"], n - 1)
                        elif exists(m):
                            pe.wait_ge(c["xct"], m + 1)
                        for kk in range(PAIRS):
                            mm(bank[7][:, 0:P], OT[:, q, kk, :], wout[:, kk, :], start=(kk == 0), stop=False)
                        mm(bank[7][:, 0:P], ones3[:], brow[:, 2, :], start=False, stop=True).then_inc(c["o"], 1)
                    if k == 3 and exists(m):
                        project_v(1)
            over_steps(pe, step1, -2, NB + 1, 3)


_INS = ["x", "ctx_1024", "mask_BxS2_bf1", "mask_BxS_ik0", "L0_xattn_Wq", "L0_xattn_bq", "L0_xattn_Wk", "L0_xattn_bk",
        "L0_xattn_Wv", "L0_xattn_bv", "L0_xattn_Wo", "L0_xattn_bo", "L0_ffn_w_gate", "L0_ffn_w1", "L0_ffn_w2",
        "L1_xattn_Wq", "L1_xattn_Wkv", "L1_xattn_Wout", "L1_xattn_bout", "L1_ffn_w1", "L1_ffn_b1", "L1_ffn_w2", "L1_ffn_b2"]


def kernel(**inputs):
    import numpy as _np
    import concourse.bacc as _bacc
    from concourse.bass_utils import run_bass_kernel_spmd as _run

    nc = _bacc.Bacc("TRN2", target_bir_lowering=False, num_devices=1)
    arrays, args = {}, []
    for name in _INS:
        a = _np.ascontiguousarray(inputs[name])
        arrays[f"in_{name}_dram"] = a
        args.append(nc.dram_tensor(f"in_{name}_dram", a.shape, mybir.dt.from_np(a.dtype), kind="ExternalInput").ap())
    args.append(nc.dram_tensor("out_0_dram", (NB, P, P), FP32, kind="ExternalOutput").ap())
    args.append(nc.dram_tensor("query_mask_parts", (NB, 3, P), BF16, kind="Internal").ap())
    for name, rows in (("expert_inputs", NE * REGION), ("expert_outputs", MAX_TILES * TILE)):
        args.append(nc.dram_tensor(name, (rows, P), FP32, kind="Internal").ap())
    build(nc, *args)
    r = _run(nc, [arrays], core_ids=[0])
    return r.results[0]["out_0_dram"]
```
